# Optimizing a Trainium2 kernel written in Bass

```python
import numpy as np
import jax
import jax.numpy as jnp

def _softmax(x, axis=-1):
    return jax.nn.softmax(x, axis=axis)

def _gelu(x):
    return jax.nn.gelu(x, approximate=True)

def _silu(x):
    return jax.nn.silu(x)

def _sigmoid(x):
    return jax.nn.sigmoid(x)

def _layernorm(x, axis=-1, eps=1e-05):
    m = jnp.mean(x, axis=axis, keepdims=True)
    v = jnp.var(x, axis=axis, keepdims=True)
    return (x - m) / jnp.sqrt(v + eps)

def _scatter_add(tgt, idx, src, axis=0):
    return tgt.at[idx].add(src)

def _segment_sum(src, seg, n):
    return jax.ops.segment_sum(src, seg, n)
kernel_name = 'mk_prb_d1_jaxref_r8_3ff0d7'

def setup_inputs(seed: int=0):
    np.random.seed(seed)
    _w = jnp.asarray

    def _L0_attn_setup():
        import jax, jax.numpy as jnp
        import numpy as np
        D_MODEL = 128
        N_HEADS = 16
        N_GROUPS = 4
        D_HEAD = D_MODEL // N_HEADS
        HPG = N_HEADS // N_GROUPS
        B, T = (2, 256)

        def _rope(x):
            t, d = (x.shape[2], x.shape[3])
            pos = jnp.arange(t, dtype=jnp.float32)[:, None]
            freq = jnp.exp(-(jnp.arange(0, d, 2, dtype=jnp.float32) / d) * jnp.log(jnp.float32(10000.0)))
            angle = pos * freq
            cos, sin = (jnp.cos(angle), jnp.sin(angle))
            xe, xo = (x[..., ::2], x[..., 1::2])
            re = xe * cos - xo * sin
            ro = xe * sin + xo * cos
            return jnp.stack([re, ro], axis=-1).reshape(x.shape)
        key = jax.random.key(seed)
        ks = jax.random.split(key, 10)
        s = 0.02
        return {'x': jax.random.normal(ks[0], (B, T, D_MODEL), dtype=jnp.float32), 'Wq': jax.random.normal(ks[1], (D_MODEL, D_MODEL), dtype=jnp.float32) * s, 'bq': jax.random.normal(ks[2], (D_MODEL,), dtype=jnp.float32) * s, 'Wk': jax.random.normal(ks[3], (D_MODEL, N_GROUPS * D_HEAD), dtype=jnp.float32) * s, 'bk': jax.random.normal(ks[4], (N_GROUPS * D_HEAD,), dtype=jnp.float32) * s, 'Wv': jax.random.normal(ks[5], (D_MODEL, N_GROUPS * D_HEAD), dtype=jnp.float32) * s, 'bv': jax.random.normal(ks[6], (N_GROUPS * D_HEAD,), dtype=jnp.float32) * s, 'Wo': jax.random.normal(ks[7], (D_MODEL, D_MODEL), dtype=jnp.float32) * s, 'bo': jax.random.normal(ks[8], (D_MODEL,), dtype=jnp.float32) * s}
    _L0_attn_in = _L0_attn_setup()

    def _L0_ffn_setup():
        import jax, jax.numpy as jnp
        import numpy as np
        B, S, H, DFF, E, K = (2, 256, 128, 256, 8, 2)

        def _moe(x, Wg, W1, b1, W2, b2, W3, b3):
            Bm, Sm, Hm = x.shape
            xt = x.reshape(-1, Hm)
            gout = xt @ Wg.T
            topv, topi = jax.lax.top_k(gout, K)
            w = jax.nn.softmax(topv, axis=-1)
            comb = jnp.einsum('tke,tk->te', jax.nn.one_hot(topi, E, dtype=x.dtype), w)
            g = jnp.einsum('th,efh->etf', xt, W1) + b1[:, None, :]
            v = jnp.einsum('th,efh->etf', xt, W2) + b2[:, None, :]
            h = jax.nn.silu(g) * v
            eo = jnp.einsum('etf,ehf->eth', h, W3) + b3[:, None, :]
            out = jnp.einsum('eth,te->th', eo, comb)
            return out.reshape(Bm, Sm, Hm)
        key = jax.random.key(seed)
        ks = jax.random.split(key, 8)
        sc_h = 1.0 / np.sqrt(H)
        sc_f = 1.0 / np.sqrt(DFF)
        x = jax.random.normal(ks[0], (B, S, H), dtype=jnp.float32)
        Wg = jax.random.uniform(ks[1], (E, H), jnp.float32, -sc_h, sc_h)
        W1 = jax.random.uniform(ks[2], (E, DFF, H), jnp.float32, -sc_h, sc_h)
        b1 = jax.random.uniform(ks[3], (E, DFF), jnp.float32, -sc_h, sc_h)
        W2 = jax.random.uniform(ks[4], (E, DFF, H), jnp.float32, -sc_h, sc_h)
        b2 = jax.random.uniform(ks[5], (E, DFF), jnp.float32, -sc_h, sc_h)
        W3 = jax.random.uniform(ks[6], (E, H, DFF), jnp.float32, -sc_f, sc_f)
        b3 = jax.random.uniform(ks[7], (E, H), jnp.float32, -sc_f, sc_f)
        return {'x': x, 'Wg': Wg, 'W1': W1, 'b1': b1, 'W2': W2, 'b2': b2, 'W3': W3, 'b3': b3}
    _L0_ffn_in = _L0_ffn_setup()
    _d = {'L0_attn_x': _L0_attn_in['x'], 'L0_attn_Wq': _L0_attn_in['Wq'], 'L0_attn_bq': _L0_attn_in['bq'], 'L0_attn_Wk': _L0_attn_in['Wk'], 'L0_attn_bk': _L0_attn_in['bk'], 'L0_attn_Wv': _L0_attn_in['Wv'], 'L0_attn_bv': _L0_attn_in['bv'], 'L0_attn_Wo': _L0_attn_in['Wo'], 'L0_attn_bo': _L0_attn_in['bo'], 'L0_ffn_Wg': _L0_ffn_in['Wg'], 'L0_ffn_W1': _L0_ffn_in['W1'], 'L0_ffn_b1': _L0_ffn_in['b1'], 'L0_ffn_W2': _L0_ffn_in['W2'], 'L0_ffn_b2': _L0_ffn_in['b2'], 'L0_ffn_W3': _L0_ffn_in['W3'], 'L0_ffn_b3': _L0_ffn_in['b3']}
    _x0 = _d['L0_attn_x']
    _d['L0_attn_x'] = jax.random.normal(jax.random.fold_in(jax.random.key(seed), 1), (2, 1024, 128), dtype=_x0.dtype)
    del _x0
    return _d

def reference(L0_attn_x, L0_attn_Wq, L0_attn_bq, L0_attn_Wk, L0_attn_bk, L0_attn_Wv, L0_attn_bv, L0_attn_Wo, L0_attn_bo, L0_ffn_Wg, L0_ffn_W1, L0_ffn_b1, L0_ffn_W2, L0_ffn_b2, L0_ffn_W3, L0_ffn_b3):

    def _L0_attn_ref(x, Wq, bq, Wk, bk, Wv, bv, Wo, bo):
        import jax, jax.numpy as jnp
        import numpy as np
        D_MODEL = 128
        N_HEADS = 16
        N_GROUPS = 4
        D_HEAD = D_MODEL // N_HEADS
        HPG = N_HEADS // N_GROUPS
        B, T = (2, 256)

        def _rope(x):
            t, d = (x.shape[2], x.shape[3])
            pos = jnp.arange(t, dtype=jnp.float32)[:, None]
            freq = jnp.exp(-(jnp.arange(0, d, 2, dtype=jnp.float32) / d) * jnp.log(jnp.float32(10000.0)))
            angle = pos * freq
            cos, sin = (jnp.cos(angle), jnp.sin(angle))
            xe, xo = (x[..., ::2], x[..., 1::2])
            re = xe * cos - xo * sin
            ro = xe * sin + xo * cos
            return jnp.stack([re, ro], axis=-1).reshape(x.shape)
        b, t, _ = x.shape
        q = (x @ Wq + bq).reshape(b, t, N_HEADS, D_HEAD).transpose(0, 2, 1, 3)
        k = (x @ Wk + bk).reshape(b, t, N_GROUPS, D_HEAD).transpose(0, 2, 1, 3)
        v = (x @ Wv + bv).reshape(b, t, N_GROUPS, D_HEAD).transpose(0, 2, 1, 3)
        k = jnp.repeat(k, HPG, axis=1)
        v = jnp.repeat(v, HPG, axis=1)
        q = _rope(q)
        k = _rope(k)
        scale = jnp.float32(np.sqrt(D_HEAD))
        scores = jnp.einsum('bhtd,bhsd->bhts', q, k) / scale
        causal = jnp.tril(jnp.ones((t, t), dtype=bool))
        scores = jnp.where(causal, scores, -jnp.inf)
        probs = jax.nn.softmax(scores, axis=-1)
        attn = jnp.einsum('bhts,bhsd->bhtd', probs, v)
        out = attn.transpose(0, 2, 1, 3).reshape(b, t, N_HEADS * D_HEAD)
        return out @ Wo + bo

    def _L0_ffn_ref(x, Wg, W1, b1, W2, b2, W3, b3):
        import jax, jax.numpy as jnp
        import numpy as np
        B, S, H, DFF, E, K = (2, 256, 128, 256, 8, 2)

        def _moe(x, Wg, W1, b1, W2, b2, W3, b3):
            Bm, Sm, Hm = x.shape
            xt = x.reshape(-1, Hm)
            gout = xt @ Wg.T
            topv, topi = jax.lax.top_k(gout, K)
            w = jax.nn.softmax(topv, axis=-1)
            comb = jnp.einsum('tke,tk->te', jax.nn.one_hot(topi, E, dtype=x.dtype), w)
            g = jnp.einsum('th,efh->etf', xt, W1) + b1[:, None, :]
            v = jnp.einsum('th,efh->etf', xt, W2) + b2[:, None, :]
            h = jax.nn.silu(g) * v
            eo = jnp.einsum('etf,ehf->eth', h, W3) + b3[:, None, :]
            out = jnp.einsum('eth,te->th', eo, comb)
            return out.reshape(Bm, Sm, Hm)
        return _moe(x, Wg, W1, b1, W2, b2, W3, b3)
    x = L0_attn_x
    xn = _layernorm(x, axis=-1)
    x = x + _L0_attn_ref(xn, L0_attn_Wq, L0_attn_bq, L0_attn_Wk, L0_attn_bk, L0_attn_Wv, L0_attn_bv, L0_attn_Wo, L0_attn_bo) + _L0_ffn_ref(xn, L0_ffn_Wg, L0_ffn_W1, L0_ffn_b1, L0_ffn_W2, L0_ffn_b2, L0_ffn_W3, L0_ffn_b3)
    return x

_drawn_inputs = setup_inputs


def setup_inputs(seed=0):
    import zlib

    import numpy as np

    out = dict(_drawn_inputs(seed))
    spreads = {}
    factors = {'L0_attn_Wq': 8.0,
     'L0_attn_bq': 8.0,
     'L0_attn_Wk': 8.0,
     'L0_attn_bk': 8.0,
     'L0_attn_Wv': 8.0,
     'L0_attn_bv': 8.0,
     'L0_attn_Wo': 8.0,
     'L0_attn_bo': 2.709,
     'L0_ffn_b1': 8.0,
     'L0_ffn_b2': 8.0,
     'L0_ffn_b3': 4.187}
    for name, (base, spread) in spreads.items():
        noise = np.random.default_rng([zlib.crc32(name.encode()), seed]).standard_normal(out[name].shape)
        drawn = base * np.exp(spread * noise) if base else spread * noise
        out[name] = jnp.asarray(drawn.astype(out[name].dtype))
    for name, factor in factors.items():
        out[name] = (out[name] * factor).astype(out[name].dtype)
    return out
```

```python
from contextlib import ExitStack

import concourse.bass as bass
from concourse import mybir

ALU = mybir.AluOpType
ACT = mybir.ActivationFunctionType
F32 = mybir.dt.float32
F32R = mybir.dt.float32r
BF16 = mybir.dt.bfloat16
AX_X = mybir.AxisListType.X

P = 128
B, T, D = 2, 1024, 128
HEADS, GROUPS, DH = 16, 4, 8
HPG = HEADS // GROUPS
E, DFF = 8, 256
TB = T // P
NTB = B * TB
NG = B * GROUPS
EPS = 1e-5
MASKED = -1e30
PARTS = 3
M_ROW = PARTS * PARTS * DH

PACK = {}
_at = 0
for _name, _n in (("Wq", 128), ("Wqr", 128), ("Wk", 32), ("Wkr", 32), ("Wvg", 40), ("bq", 1), ("bqr", 1), ("bk", 1),
                  ("bkr", 1), ("bv", 32), ("Wo", 128), ("bo", 128), ("b3", 128)):
    PACK[_name] = (_at, _at + _n)
    _at += _n
PACK_N = _at
CONST = {}
_at = 0
for _name, _n in (("ident", 128), ("cosk", 512), ("sink", 512), ("prio", 8), ("cosq", 1024), ("sinq", 1024),
                  ("mask", 512)):
    CONST[_name] = (_at, _at + _n)
    _at += _n
CONST_N = _at
CONST_FIRST = CONST["cosq"][0]

UNITS = 36
STEPS = 10
STEP_PARTS = [
    [(0, 0, 512)],
    [(1, 128, 384), (3, 384, 128)],
    [(2, 256, 256)],
    [(0, 512, 512)],
    [(1, 512, 512)],
    [(2, 512, 512)],
    [(3, 512, 512)],
    [(4, 512, 512)],
    [(5, 640, 384), (7, 896, 128)],
    [(6, 768, 256)],
]
P_UNITS = []
STEP_LAST_UNIT = []
STEP_OF_UNIT = []
for _s, _parts in enumerate(STEP_PARTS):
    if sum(p[2] for p in _parts) == 512:
        for _h in range(HPG):
            _c = 0
            _u = []
            for _j, _t0, _n in _parts:
                _u.append((_h, _j, _t0, _n, _c))
                _c += _n
            P_UNITS.append(_u)
            STEP_OF_UNIT.append(_s)
    else:
        _j, _t0, _n = _parts[0]
        for _h in (0, 2):
            P_UNITS.append([(_h, _j, _t0, _n, 0), (_h + 1, _j, _t0, _n, _n)])
            STEP_OF_UNIT.append(_s)
    STEP_LAST_UNIT.append(len(P_UNITS) - 1)
assert len(P_UNITS) == UNITS
HAS_DIAGONAL = [any(t0 == j * P for j, t0, n in parts) for parts in STEP_PARTS]
MASKS = sum(HAS_DIAGONAL)
S_UNITS = []
for _h in range(HPG):
    for _i in (3, 4, 5, 6, 7):
        S_UNITS.append([(_h, _i, 0, 512, 0)])
    S_UNITS.append([(_h, 7, 512, 512, 0)])
    S_UNITS.append([(_h, 0, 0, 128, 0), (_h, 2, 0, 384, 128)])
    S_UNITS.append([(_h, 4, 512, 128, 0), (_h, 6, 512, 384, 128)])
    S_UNITS.append([(_h, 1, 0, 256, 0), (_h, 5, 512, 256, 256)])
assert len(S_UNITS) == UNITS
RING_PER_GROUP = UNITS + 3
CHUNKS = 8
CHUNK = B * T // CHUNKS

POSITIONS = 40
PV_AT = {6: 0, 10: 1, 12: 2, 16: 3, 20: 4, 24: 5, 28: 6, 32: 7, 36: 8, 38: 9}
EVAC_AT = {14: 0, 38: 1}
OT_AT = {17: 0, 39: 1}
M_AT = 33
MOE_ITEMS = []
for _c in range(CHUNKS):
    MOE_ITEMS += [(_c, "up0"), (_c, "up1")] + ([(_c - 1, "down")] if _c else [])
MOE_ITEMS.append((CHUNKS - 1, "down"))
MOE_INDEX = {_item: _i for _i, _item in enumerate(MOE_ITEMS)}


def _spread(first, last, n):
    at = {}
    span = last - first + 1
    for i in range(n):
        at.setdefault(first + i * span // n, []).append(i)
    return at


S_AT = _spread(5, 31, UNITS)
MOE_AT = {}
for _i, _item in enumerate(MOE_ITEMS):
    MOE_AT.setdefault(_i * (POSITIONS - 3) // (len(MOE_ITEMS) - 1), []).append(_item)
SPLIT_AT = {3: 0, 9: 1, 15: 2, 21: 3}
QUARTER = 2 * DFF // 4


def up_count(c, f):
    return 2 * c + f + 1


TAIL_AT = {0: [("comb", 0, 0)], 2: [("comb", 0, 1)], 4: [("comb", 0, 2)], 6: [("comb", 0, 3)], 8: [("turn", 0, 0)],
           10: [("turn", 0, 1)], 12: [("project", 0, 0)], 14: [("project", 0, 1)], 20: [("turn", 1, 0)],
           23: [("project", 1, 0)]}
TAIL_END = [("turn", 1, 1), ("project", 1, 1)]
TAIL_INDEX = {}
_i = 0
for _p in range(POSITIONS):
    for _w in TAIL_AT.get(_p, []) + ([("outputs", 1, OT_AT[_p])] if _p in OT_AT else []):
        TAIL_INDEX[_w] = _i
        _i += 1
for _w in TAIL_END:
    TAIL_INDEX[_w] = _i
    _i += 1


def attention_and_experts(nc, x, pack, const, wa, wd, zrow, out):
    q_dram = nc.dram_tensor("q_parts", (NG, PARTS, DH, HPG * T), BF16).ap()
    k_dram = nc.dram_tensor("k_parts", (NG, PARTS, DH, T), BF16).ap()

    with ExitStack() as ctx:
        def sb(name, shape, dt=F32):
            return ctx.enter_context(nc.sbuf_tensor(name, shape, dt))

        def sem(name):
            return ctx.enter_context(nc.semaphore(name))

        pk = sb("pk", [P, PACK_N])
        cn = sb("cn", [P, CONST_N])
        xs = sb("xs", [P, NTB, D])
        acc = sb("acc", [P, NTB, D])
        stats = sb("stats", [P, NTB, 6])
        meanvar = sb("meanvar", [P, NTB, 2])
        rstd = sb("rstd", [P, NTB])
        deviation = sb("deviation", [P, NTB])
        xT = sb("xT", [P, B * T])
        xh = sb("xh", [P, B * T], F32R)
        xl = sb("xl", [P, B * T], F32R)
        q_part = sb("q_part", [P, PARTS, T], BF16)
        krope_a = sb("krope_a", [P, 512])
        krope_b = sb("krope_b", [P, 512])
        k_part = sb("k_part", [P, PARTS, 512], BF16)
        qs = sb("qs", [P, 2, HPG * T], BF16)
        ks = sb("ks", [P, 2, T], BF16)
        vt = sb("vt", [P, NG, TB, 32])
        vcur = sb("vcur", [P, 2, TB, 32])
        pt = sb("pt", [P, 4, HPG * 512])
        rope_a, rope_b = pt[:, 3, 0:T], pt[:, 3, T:2 * T]
        junk = sb("junk", [P, 4, 512])
        mx = sb("mx", [P, HPG, TB])
        mx_a = sb("mx_a", [P, HPG, 4])
        mx_b = sb("mx_b", [P, HPG, 4])
        mrow = sb("mrow", [HPG * TB, PARTS, P], BF16)
        mres = sb("mres", [HPG * TB, 2, P])
        o_t = sb("o_t", [P, 2, 512])
        rl = sb("rl", [P, 2, 16])
        on = sb("on", [P, TB, NG // 2, 2 * HPG * DH])
        xn = sb("xn", [P, NTB, D])
        on_t = xn[:, :, :].rearrange("p (b i) c -> p b i c", b=B)
        gate = sb("gate", [P, NTB, E])
        gtmp = sb("gtmp", [P, 5, NTB, E])
        gcol = sb("gcol", [P, 6, NTB])
        comb = sb("comb", [P, E, NTB])
        comb_cur = sb("comb_cur", [P, 2, NTB])
        comb_t = sb("comb_t", [E, B * T])
        w_raw = sb("w_raw", [P, 2, 2 * DFF + 4])
        w_h = sb("w_h", [P, 2, 2 * DFF], F32R)
        w_l = sb("w_l", [P, 2, 2 * DFF], F32R)
        w_down = sb("w_down", [P, 2, 2 * D])
        half_b1 = sb("half_b1", [P, 2, 2])
        th = sb("th", [P, 2, 2, CHUNK])
        zz = sb("zz", [P, 2, CHUNK])
        h_part = sb("h_part", [P, 2, CHUNK])
        hh = sb("hh", [P, 2, 2, CHUNK])
        bank = [ctx.enter_context(nc.psum_tensor(f"bank{i}", [P, 512], F32)) for i in range(8)]
        p_bank = bank[0:2]
        r_bank = bank[2:4]
        o_bank = bank[4:6]
        m_bank = bank[6:8]

        def pkc(name, rows=P):
            a, b = PACK[name]
            return pk[0:rows, a:b]

        def cnc(name):
            a, b = CONST[name]
            return cn[:, a:b]

        ident = cnc("ident")

        x_loaded = [sem(f"x_loaded{b}") for b in range(B)]
        pack_loaded = sem("pack_loaded")
        const_loaded = sem("const_loaded")
        tables_loaded = sem("tables_loaded")
        var_due = sem("var_due")
        deviation_done = sem("deviation_done")
        xn_done = sem("xn_done")
        xT_made = sem("xT_made")
        xT_done = sem("xT_done")
        xh_done = sem("xh_done")
        xl_done = sem("xl_done")
        q_made = sem("q_made")
        q_taken = sem("q_taken")
        k_made = sem("k_made")
        vg_made = sem("vg_made")
        part_due = sem("part_due")
        part_done = sem("part_done")
        q_stored = [sem(f"q_stored{b}") for b in range(B)]
        k_stored = sem("k_stored")
        gate_due = sem("gate_due")
        gate_exp = sem("gate_exp")
        v_made = sem("v_made")
        comb_done = sem("comb_done")
        acc_begun = sem("acc_begun")
        cleared = sem("cleared")
        own = sem("own")
        stack_loaded = sem("stack_loaded")
        v_loaded = sem("v_loaded")
        w_loaded = [sem(f"w_loaded{par}") for par in range(2)]
        w_split = sem("w_split")
        m_loaded = sem("m_loaded")
        minus_loaded = sem("minus_loaded")
        p_full = sem("p_full")
        exp_done = sem("exp_done")
        mask_done = sem("mask_done")
        pv_step = sem("pv_step")
        o_copied = sem("o_copied")
        r_full = sem("r_full")
        r_free = sem("r_free")
        mx_done = sem("mx_done")
        mrow_done = sem("mrow_done")
        up_made = sem("up_made")
        act_made = sem("act_made")
        factor_made = sem("factor_made")
        h_begun = sem("h_begun")
        h_made = sem("h_made")
        down_made = sem("down_made")
        acc_added = sem("acc_added")
        stored = sem("stored")
        P_CREDIT, R_CREDIT, PT_CREDIT, O_CREDIT, ACC_CREDIT = 2, 2, 4, 2, 2

        waited = sem("waited")
        STACK_DMAS = PARTS * PARTS + PARTS + 1

        block = ctx.enter_context(nc.Block())

        def wait_apart(eng, semaphore, value):
            eng.wait_ge(semaphore, value)
            eng.sem_inc(waited, 1)

        @block.sync
        def _(sp):
            def load_stack(m, par):
                for a in range(PARTS):
                    for b in range(PARTS):
                        r = (a * PARTS + b) * DH
                        sp.dma_start(qs[r:r + DH, par, :], q_dram[bass.ds(m, 1), a].rearrange("o d t -> (o d) t"))\
                            .then_inc(stack_loaded, 16)
                    r = a * PARTS * DH
                    sp.dma_start(ks[r:r + PARTS * DH, par, :],
                                 k_dram[bass.ds(m, 1)].rearrange("o a d t -> (o a d) t")).then_inc(stack_loaded, 16)
                sp.dma_start(qs[M_ROW:M_ROW + PARTS, par, :], zrow[0:PARTS, :]).then_inc(stack_loaded, 16)

            def load_v(m, par):
                sp.dma_start(vcur[:, par].rearrange("p j c -> p (j c)"),
                             vt[:, bass.ds(m, 1)].rearrange("p o j c -> p (o j c)")).then_inc(v_loaded, 16)

            def load_expert(m, par):
                sp.dma_start(w_raw[:, par, :], wa[bass.ds(m, 1)].rearrange("o p c -> (o p) c")).then_inc(w_loaded[par], 16)
                sp.dma_start(w_down[:, par, :], wd[bass.ds(m, 1)].rearrange("o p c -> (o p) c")).then_inc(w_loaded[par], 16)

            def load_maxima(m, par):
                sp.wait_ge(mrow_done, m + 1)
                for c in range(PARTS):
                    sp.dma_start(qs[M_ROW + c:M_ROW + c + 1, par, :], mrow[:, c, :]).then_inc(m_loaded, 16)

            def group(n, half, experts):
                sp.wait_ge(exp_done, n * UNITS + P_CREDIT)
                load_stack(n + 1, 1 - half)
                sp.wait_ge(pv_step, n * STEPS + PT_CREDIT)
                load_v(n + 1, 1 - half)
                if experts:
                    sp.wait_ge(acc_added, n * CHUNKS + CHUNKS + ACC_CREDIT)
                    load_expert(n + 2, half)
                load_maxima(n + 1, 1 - half)

            for b in range(B):
                sp.dma_start(xs[:, b * TB:(b + 1) * TB, :], x[b].rearrange("(i p) c -> p i c", p=P))\
                    .then_inc(x_loaded[b], 16)
            sp.dma_start(pk[:, :], pack).then_inc(pack_loaded, 16)
            for e in range(2):
                load_expert(e, e)
            sp.wait_ge(cleared, 2)
            for par in range(2):
                sp.dma_start(ks[M_ROW:M_ROW + PARTS, par, :], zrow[PARTS:2 * PARTS, 0:T]).then_inc(minus_loaded, 16)
            sp.wait_ge(part_done, 3)
            for a in range(PARTS):
                for c in range(4):
                    b, half = c // 2, c % 2
                    dst = k_dram[GROUPS * b:GROUPS * (b + 1), a, :, half * 512:(half + 1) * 512]
                    sp.dma_start(dst, k_part[32 * c:32 * (c + 1), a, :]).then_inc(k_stored, 16)
            sp.wait_ge(k_stored, 16 * 12)
            for b in range(B):
                sp.wait_ge(part_done, 3 * (b + 2))
                for g in range(GROUPS):
                    for a in range(PARTS):
                        dst = q_dram[GROUPS * b + g, a].rearrange("d (h t) -> h d t", h=HPG)
                        sp.dma_start(dst, q_part[32 * g:32 * (g + 1), a, :]).then_inc(q_stored[b], 16)
                if b == 0:
                    sp.wait_ge(q_stored[0], 16 * GROUPS * PARTS)
                    load_stack(0, 0)
                    sp.wait_ge(v_made, 2)
                    load_v(0, 0)
            sp.wait_ge(q_stored[1], 16 * GROUPS * PARTS)
            load_maxima(0, 0)
            with sp.Fori(0, NG // 2 - 1) as k:
                for half in range(2):
                    group(2 * k + half, half, True)
            group(NG - 2, 0, False)
            for b in range(B):
                for i in range(2):
                    sp.wait_ge(r_free, NG * RING_PER_GROUP + TAIL_INDEX["project", b, i] + 1 + R_CREDIT)
                    sp.dma_start(out[b, 512 * i:512 * (i + 1)].rearrange("(i p) c -> p i c", p=P),
                                 acc[:, TB * b + 4 * i:TB * b + 4 * i + 4, :]).then_inc(stored, 16)
            sp.wait_ge(stored, 16 * B * 2)

        @block.gpsimd
        def _(pool):
            def split_expert(m, par, turn):
                wait_apart(pool, w_loaded[par], 32 * (turn + 1))
                pool.tensor_copy(w_h[:, par, :], w_raw[:, par, 0:2 * DFF]).then_inc(w_split, 1)
                pool.tensor_scalar(half_b1[:, par, :], w_raw[:, par, 2 * DFF:2 * DFF + 2], 0.5, None, ALU.mult)\
                    .then_inc(w_split, 1)
                pool.tensor_copy(comb_cur[:, par, :], comb[:, bass.ds(m, 1), :].rearrange("p o i -> p (o i)"))\
                    .then_inc(w_split, 1)
                pool.wait_ge(w_split, 4 * m + 1)
                pool.tensor_tensor(w_l[:, par, :], w_raw[:, par, 0:2 * DFF], w_h[:, par, :].bitcast(F32),
                                   ALU.subtract).then_inc(w_split, 1)

            def mask(n, half, s):
                wait_apart(pool, exp_done, n * UNITS + STEP_LAST_UNIT[s] + 1 + P_CREDIT)
                width = sum(w for _, _, w in STEP_PARTS[s])
                c = 0
                for _, _, w in STEP_PARTS[s]:
                    v = pt[:, (half * STEPS + s) % 4, 0:HPG * width].rearrange("p (h c) -> p h c", h=HPG)[:, :, c:c + P]
                    ins = pool.affine_select(out=v, in_=v, compare_op=ALU.is_ge, fill=0.0, base=0,
                                             pattern=[[0, HPG], [1, P]], channel_multiplier=-1)
                    c += w
                ins.then_inc(mask_done, 1)

            def expert_h(m, c, f):
                h = hh[:, c % 2, f, :]
                pool.wait_ge(factor_made, m * 2 * CHUNKS + up_count(c, f))
                pool.tensor_tensor(h_part[:, f, :], th[:, c % 2, f, :], h, ALU.mult).then_inc(h_begun, 1)
                pool.wait_ge(h_begun, m * 2 * CHUNKS + up_count(c, f))
                pool.tensor_tensor(h, h_part[:, f, :], h, ALU.add).then_inc(h_made, 1)

            def group(n, half, front, k=None):
                for pos in range(POSITIONS):
                    for s in range(STEPS):
                        if STEP_LAST_UNIT[s] == pos and HAS_DIAGONAL[s]:
                            mask(n, half, s)
                    if front:
                        for c, kind in MOE_AT.get(pos, []):
                            if kind != "down":
                                expert_h(n + 1, c, int(kind[2]))
                    if k is not None and pos == 12:
                        split_expert(n + 2, half, k + 1)

            pool.memset(qs[:, :, :].bitcast(F32), 0.0).then_inc(cleared, 1)
            pool.memset(ks[:, :, :].bitcast(F32), 0.0).then_inc(cleared, 1)
            pool.memset(vt[:, :, :, :], 0.0).then_inc(cleared, 1)
            pool.wait_ge(cleared, 3)
            pool.memset(vt[:, :, :, DH:DH + 1], 1.0).then_inc(cleared, 1)
            for b in range(B):
                pool.wait_ge(x_loaded[b], 16)
            pool.wait_ge(pack_loaded, 16)
            pool.tensor_tensor(acc[:, :, :], xs[:, :, :], pkc("bo").unsqueeze(1).to_broadcast([P, NTB, D]), ALU.add)\
                .then_inc(acc_begun, 1)
            for i in range(4):
                pool.wait_ge(xh_done, i + 1)
                pool.tensor_tensor(xl[:, 512 * i:512 * (i + 1)], xT[:, 512 * i:512 * (i + 1)],
                                   xh[:, 512 * i:512 * (i + 1)].bitcast(F32), ALU.subtract).then_inc(xl_done, 1)
            pool.wait_ge(comb_done, 1)
            for e in range(2):
                split_expert(e, e, 0)
            for c in range(CHUNKS):
                for f in range(2):
                    expert_h(0, c, f)
            with pool.Fori(0, NG // 2 - 1) as k:
                for half in range(2):
                    group(2 * k + half, half, True, k)
            group(NG - 2, 0, True)
            group(NG - 1, 1, False)

        @block.scalar
        def _(act):
            def exp_unit(n, half, u):
                s = STEP_OF_UNIT[u]
                first = STEP_LAST_UNIT[s - 1] + 1 if s else 0
                if u == first:
                    act.wait_ge(pv_step, n * STEPS + s + 1)
                act.wait_ge(p_full, n * UNITS + u + 1)
                at = (u - first) * 512
                nc.scalar.activation(pt[:, (half * STEPS + s) % 4, at:at + 512], p_bank[u % 2][:, :], ACT.Exp)\
                    .then_inc(exp_done, 1)

            def expert_act(m, par, c, f):
                act.wait_ge(up_made, m * 2 * CHUNKS + 2 * c + f + 1)
                src = m_bank[MOE_INDEX[c, f"up{f}"] % 2][:, 0:CHUNK]
                nc.scalar.activation(th[:, c % 2, f, :], src, ACT.Tanh, bias=half_b1[:, par, f:f + 1], scale=0.5)
                nc.scalar.activation(zz[:, f, :], src, ACT.Identity, bias=half_b1[:, par, f:f + 1], scale=0.5)\
                    .then_inc(act_made, 1)

            def copy_outputs(n, x):
                act.wait_ge(pv_step, n * STEPS + (3, STEPS)[x] + PT_CREDIT)
                nc.scalar.copy(o_t[:, x, :], o_bank[x][:, :]).then_inc(o_copied, 1)

            def group(n, half, front):
                for pos in range(POSITIONS):
                    if pos < UNITS:
                        exp_unit(n, half, pos)
                    if front:
                        for c, kind in MOE_AT.get(pos, []):
                            if kind != "down":
                                expert_act(n + 1, 1 - half, c, int(kind[2]))
                    if pos in EVAC_AT:
                        copy_outputs(n, EVAC_AT[pos])

            act.dma_start(cn[:, 0:CONST_FIRST], const[:, 0:CONST_FIRST]).then_inc(const_loaded, 16)
            act.dma_start(cn[:, CONST_FIRST:CONST_N], const[:, CONST_FIRST:CONST_N]).then_inc(tables_loaded, 16)
            act.sem_inc(exp_done, P_CREDIT)
            act.sem_inc(o_copied, O_CREDIT)
            for b in range(B):
                act.wait_ge(var_due, b + 1)
                nc.scalar.activation(deviation[:, TB * b:TB * (b + 1)], rstd[:, TB * b:TB * (b + 1)], ACT.Sqrt)\
                    .then_inc(deviation_done, 1)
            for i in range(4):
                act.wait_ge(xT_made, i + 1)
                nc.scalar.copy(xT[:, 512 * i:512 * (i + 1)], bank[i][:, :]).then_inc(xT_done, 1)
            for i in range(3):
                for a in range(PARTS):
                    act.wait_ge(part_due, 3 * i + a + 1)
                    src, dst = (krope_a, k_part[:, a, :]) if i == 0 else (rope_a, q_part[:, a, :])
                    if i == 2 and a == 0:
                        act.wait_ge(q_stored[0], 16 * GROUPS * PARTS)
                    nc.scalar.copy(dst, src[:, :]).then_inc(part_done, 1)
                if i == 1:
                    act.wait_ge(gate_due, 1)
                    nc.scalar.activation(gcol[:, 3, :], gcol[:, 2, :], ACT.Exp).then_inc(gate_exp, 1)
            for c in range(CHUNKS):
                for f in range(2):
                    expert_act(0, 0, c, f)
            with act.Fori(0, NG // 2 - 1) as k:
                for half in range(2):
                    group(2 * k + half, half, True)
            group(NG - 2, 0, True)
            group(NG - 1, 1, False)

        @block.vector
        def _(dve):
            steps = [0]

            def link(ins):
                ins.then_inc(own, 1)
                steps[0] += 1
                dve.wait_ge(own, steps[0])

            ring = {}

            def score_unit(m, u, r):
                wait_apart(dve, r_full, m_ring(m) + r + 1)
                b = ring_bank(m, r)
                pieces = S_UNITS[u]
                for n, (h, i, s0, w, c) in enumerate(pieces):
                    src = r_bank[b][:, c:c + w]
                    if i < 4:
                        dst = mx[:, h, i:i + 1]
                    else:
                        dst = (mx_b if s0 else mx_a)[:, h, i - 4:i - 3]
                    if s0 + w == (i + 1) * P:
                        ins = dve.tensor_tensor_reduce(junk[:, 2 * b + n, 0:w], src, cnc("mask")[:, 512 - w:512],
                                                       1.0, MASKED, ALU.add, ALU.max, dst)
                    else:
                        ins = dve.tensor_reduce(dst, src, AX_X, ALU.max)
                ins.then_inc(r_free, 1)

            def m_ring(m):
                return m * RING_PER_GROUP

            half_of = [0]

            def ring_bank(m, r):
                return (half_of[0] * RING_PER_GROUP + r) % 2

            def group_maxima(m):
                dve.wait_ge(r_free, m_ring(m) + ring["last_score"] + 1 + R_CREDIT)
                dve.tensor_tensor(mx[:, :, 4:8], mx_a[:, :, :], mx_b[:, :, :], ALU.max).then_inc(mx_done, 1)

            def maxima_rows(m, r, taken=1):
                dve.wait_ge(r_full, m_ring(m) + r + 1)
                src = r_bank[ring_bank(m, r)][0:HPG * TB, 0:P]
                base = 3 * m
                dve.tensor_copy(mrow[:, 0, :], src).then_inc(mstep, 1)
                dve.wait_ge(mstep, base + 1)
                dve.tensor_tensor(mres[:, 0, :], src, mrow[:, 0, :], ALU.subtract).then_inc(r_free, taken)
                dve.wait_ge(r_free, m_ring(m) + r + taken + R_CREDIT)
                dve.tensor_copy(mrow[:, 1, :], mres[:, 0, :]).then_inc(mstep, 1)
                dve.wait_ge(mstep, base + 2)
                dve.tensor_tensor(mres[:, 1, :], mres[:, 0, :], mrow[:, 1, :], ALU.subtract).then_inc(mstep, 1)
                dve.wait_ge(mstep, base + 3)
                dve.tensor_copy(mrow[:, 2, :], mres[:, 1, :]).then_inc(mrow_done, 1)

            mstep = sem("mstep")
            rlstep = sem("rlstep")

            def outputs(m, r, n, k, half, x):
                dve.wait_ge(r_full, m_ring(m) + r + 1)
                src = r_bank[ring_bank(m, r)][:, :].rearrange("p (i h c) -> p i h c", i=4, h=HPG)
                flat = r_bank[ring_bank(m, r)][:, :].rearrange("p (q c) -> p q c", c=32)
                dve.reciprocal(rl[:, x, :], flat[:, :, DH]).then_inc(rlstep, 1)
                dve.wait_ge(rlstep, 2 * n + x + 1)
                dst = on[:, 4 * x:4 * x + 4, bass.ds(k, 1), 32 * half:32 * half + 32]
                dst = dst.rearrange("p i o (h d) -> p (i o) h d", h=HPG)
                inv = rl[:, x, :].rearrange("p (i h) -> p i h", i=4).unsqueeze(3).to_broadcast([P, 4, HPG, DH])
                dve.tensor_tensor(dst, src[:, :, :, 0:DH], inv, ALU.mult).then_inc(r_free, 1)

            def expert_factor(m, par, c, f):
                dve.wait_ge(act_made, m * 2 * CHUNKS + up_count(c, f))
                dve.scalar_tensor_tensor(out=hh[:, c % 2, f, :],
                                         in0=m_bank[MOE_INDEX[c, f"up{f}"] % 2][:, CHUNK:2 * CHUNK],
                                         scalar=w_raw[:, par, 2 * DFF + 2 + f:2 * DFF + 3 + f], in1=zz[:, f, :],
                                         op0=ALU.add, op1=ALU.mult).then_inc(factor_made, 1)

            def expert_add(m, par, c):
                dve.wait_ge(down_made, m * CHUNKS + c + 1)
                for i in range(2):
                    t = 2 * c + i
                    ins = dve.scalar_tensor_tensor(out=acc[:, t, :], in0=m_bank[MOE_INDEX[c, "down"] % 2][:, D * i:D * (i + 1)],
                                                   scalar=comb_cur[:, par, t:t + 1], in1=acc[:, t, :],
                                                   op0=ALU.mult, op1=ALU.add)
                ins.then_inc(acc_added, 1)

            def moe(m, par, items):
                for c, kind in items:
                    if kind == "down":
                        expert_add(m, par, c)
                    else:
                        expert_factor(m, par, c, int(kind[2]))

            def due(pos):
                return ([w for w in MOE_AT.get(pos - 2, []) if w[1] != "down"]
                        + [w for w in MOE_AT.get(pos - 1, []) if w[1] == "down"])

            def group(n, k, half, front):
                m = n + 1
                half_of[0] = 1 - half if front else 0
                r = 0
                for pos in range(POSITIONS):
                    if front:
                        moe(m, 1 - half, due(pos))
                    if front:
                        for u in S_AT.get(pos, []):
                            score_unit(m, u, r)
                            ring["last_score"] = r
                            r += 1
                        if pos == M_AT - 1:
                            group_maxima(m)
                        if pos == M_AT:
                            maxima_rows(m, r)
                            r += 1
                    if pos in OT_AT:
                        outputs(m, r, n, k, half, OT_AT[pos])
                        r += 1
                if front:
                    for pos in (POSITIONS, POSITIONS + 1):
                        moe(m, 1 - half, due(pos))

            dve.sem_inc(r_free, R_CREDIT)
            dve.sem_inc(acc_added, ACC_CREDIT)
            for b in range(B):
                lo, hi = b * TB, (b + 1) * TB
                dve.wait_ge(x_loaded[b], 16)
                for i in range(lo, hi):
                    ins = dve.bn_stats(stats[:, i, :], xs[:, i, :])
                link(ins)
                for i in range(lo, hi):
                    ins = dve.bn_aggr(meanvar[:, i, :], stats[:, i, :])
                link(ins)
                dve.tensor_scalar(rstd[:, lo:hi], meanvar[:, lo:hi, 1], EPS, None, ALU.add).then_inc(var_due, 1)
                dve.wait_ge(deviation_done, b + 1)
                link(dve.reciprocal(rstd[:, lo:hi], deviation[:, lo:hi]))
                for i in range(lo, hi):
                    ins = dve.tensor_scalar(xn[:, i, :], xs[:, i, :], meanvar[:, i, 0:1], rstd[:, i:i + 1],
                                            ALU.subtract, ALU.mult)
                ins.then_inc(xn_done, 1)
            dve.wait_ge(pack_loaded, 16)
            dve.wait_ge(const_loaded, 16)

            def rope(dst_a, dst_b, made, at, bank_q, bank_r, bias, bias_r, cos, sin):
                dve.wait_ge(made, at)
                dve.scalar_tensor_tensor(out=dst_a, in0=bank_q[:, :], scalar=pkc(bias), in1=cos, op0=ALU.add,
                                         op1=ALU.mult)
                return dve.scalar_tensor_tensor(out=dst_b, in0=bank_r[:, :], scalar=pkc(bias_r), in1=sin,
                                                op0=ALU.add, op1=ALU.mult)

            def parts(i, a_buf, b_buf, part):
                dve.tensor_tensor(a_buf[:, :], a_buf[:, :], b_buf[:, :], ALU.add).then_inc(part_due, 1)
                for a in range(PARTS - 1):
                    dve.wait_ge(part_done, 3 * i + a + 1)
                    dve.tensor_tensor(a_buf[:, :], a_buf[:, :], part[:, a, :], ALU.subtract).then_inc(part_due, 1)

            link(rope(krope_a[:, :], krope_b[:, :], k_made, 1, bank[0], bank[1], "bk", "bkr", cnc("cosk"),
                      cnc("sink")))
            parts(0, krope_a, krope_b, k_part)
            dve.wait_ge(tables_loaded, 16)

            def q_of(b):
                if b:
                    dve.wait_ge(part_done, 6)
                for c in range(2):
                    ins = rope(rope_a[:, 512 * c:512 * (c + 1)], rope_b[:, 512 * c:512 * (c + 1)], q_made,
                               2 * b + c + 1, bank[4 + c], bank[6 + c], "bq", "bqr",
                               cnc("cosq")[:, 512 * c:512 * (c + 1)], cnc("sinq")[:, 512 * c:512 * (c + 1)])
                    ins.then_inc(q_taken, 1)
                dve.wait_ge(q_taken, 2 * b + 2)
                parts(1 + b, rope_a, rope_b, q_part)

            q_of(0)
            for b in range(B):
                dve.wait_ge(vg_made, b + 1)
                if b == 0:
                    dve.wait_ge(cleared, 4)
                src = bank[2 + b][:, 0:TB * 40].rearrange("p (j c) -> p j c", c=40)
                for g in range(GROUPS):
                    ins = dve.tensor_tensor(vt[:, GROUPS * b + g, :, 0:DH], src[:, :, DH * g:DH * (g + 1)],
                                            pkc("bv")[:, DH * g:DH * (g + 1)].unsqueeze(1).to_broadcast([P, TB, DH]),
                                            ALU.add)
                dve.tensor_copy(gate[:, TB * b:TB * (b + 1), :], src[:, :, 32:40]).then_inc(v_made, 1)
            dve.wait_ge(v_made, 2)

            def col(i):
                return gcol[:, i, :].unsqueeze(2).to_broadcast([P, NTB, E])

            prio = cnc("prio").unsqueeze(1).to_broadcast([P, NTB, E])
            left = gate
            for i in range(2):
                best, eq, one = gcol[:, i, :], gtmp[:, 0], gtmp[:, 1 + i]
                link(dve.tensor_reduce(best, left[:, :, :], AX_X, ALU.max))
                link(dve.tensor_tensor(eq, left[:, :, :], col(i), ALU.is_equal))
                link(dve.tensor_tensor(eq, eq, prio, ALU.mult))
                link(dve.tensor_reduce(gcol[:, 4, :], eq, AX_X, ALU.max))
                link(dve.tensor_tensor(one, eq, col(4), ALU.is_equal))
                if i == 0:
                    link(dve.scalar_tensor_tensor(out=gtmp[:, 3], in0=one, scalar=-3e38, in1=gate[:, :, :],
                                                  op0=ALU.mult, op1=ALU.add))
                    left = gtmp[:, 3]
            dve.tensor_tensor(gcol[:, 2, :], gcol[:, 1, :], gcol[:, 0, :], ALU.subtract).then_inc(gate_due, 1)
            dve.wait_ge(gate_exp, 1)
            link(dve.tensor_scalar(gcol[:, 5, :], gcol[:, 3, :], 1.0, None, ALU.add))
            link(dve.reciprocal(gcol[:, 0, :], gcol[:, 5, :]))
            link(dve.tensor_tensor(gcol[:, 1, :], gcol[:, 3, :], gcol[:, 0, :], ALU.mult))
            dve.tensor_tensor(gtmp[:, 0], gtmp[:, 1], col(0), ALU.mult)
            link(dve.tensor_tensor(gtmp[:, 4], gtmp[:, 2], col(1), ALU.mult))
            dve.tensor_tensor(comb[:, :, :].rearrange("p e i -> p i e"), gtmp[:, 0], gtmp[:, 4], ALU.add)\
                .then_inc(comb_done, 1)
            for i in range(4):
                dve.wait_ge(xT_done, i + 1)
                dve.tensor_copy(xh[:, 512 * i:512 * (i + 1)], xT[:, 512 * i:512 * (i + 1)]).then_inc(xh_done, 1)
            q_of(1)
            dve.wait_ge(acc_begun, 1)

            half_of[0] = 0
            r = 0
            moe_at = _spread(0, UNITS - 1, len(MOE_ITEMS))
            for u in range(UNITS):
                score_unit(0, u, r)
                ring["last_score"] = r
                r += 1
                if u >= 2:
                    moe(0, 0, [MOE_ITEMS[i] for i in moe_at.get(u - 2, [])])
            group_maxima(0)
            for u in (UNITS - 2, UNITS - 1):
                moe(0, 0, [MOE_ITEMS[i] for i in moe_at.get(u, [])])
            maxima_rows(0, r, RING_PER_GROUP - UNITS)

            with dve.Fori(0, NG // 2 - 1) as k:
                for half in range(2):
                    group(2 * k + half, k, half, True)
            group(NG - 2, NG // 2 - 1, 0, True)

            def tail(r, what):
                kind, b, i = what
                dve.wait_ge(r_full, m_ring(NG) + r + 1)
                src = r_bank[ring_bank(NG, r)]
                if kind == "comb":
                    ins = dve.tensor_copy(comb_t[:, 512 * i:512 * (i + 1)], src[0:E, :])
                elif kind == "turn":
                    ins = dve.tensor_copy(on_t[:, b, 4 * i:4 * i + 4, :].rearrange("p i c -> p (i c)"), src[:, :])
                else:
                    dst = acc[:, TB * b + 4 * i:TB * b + 4 * i + 4, :].rearrange("p i c -> p (i c)")
                    ins = dve.tensor_tensor(dst, dst, src[:, :], ALU.add)
                ins.then_inc(r_free, 1)

            m = NG
            half_of[0] = 0
            r = 0
            for pos in range(POSITIONS):
                for what in TAIL_AT.get(pos, []):
                    tail(r, what)
                    r += 1
                if pos in OT_AT:
                    outputs(m, r, NG - 1, NG // 2 - 1, 1, OT_AT[pos])
                    r += 1
            for what in TAIL_END:
                tail(r, what)
                r += 1

        @block.tensor
        def _(pe):
            half_of = [0]

            def ring_fill(m, r):
                pe.wait_ge(r_free, m * RING_PER_GROUP + r + 1)
                return r_bank[(half_of[0] * RING_PER_GROUP + r) % 2]

            def score_unit(m, par, u, r):
                if u == 0:
                    pe.wait_ge(stack_loaded, 16 * STACK_DMAS * (m + 1))
                dst = ring_fill(m, r)
                for h, i, s0, w, c in S_UNITS[u]:
                    q0 = h * T + i * P
                    mm = pe.matmul(dst[:, c:c + w], qs[:, par, q0:q0 + P], ks[:, par, s0:s0 + w], start=True,
                                   stop=True)
                mm.then_inc(r_full, 1)

            def turn_maxima(m, r, made=1):
                dst = ring_fill(m, r)
                pe.wait_ge(mx_done, m + 1)
                pe.transpose(dst[0:HPG * TB, 0:P], mx[:, :, :].rearrange("p h i -> p (h i)"), ident)\
                    .then_inc(r_full, made)

            def prob_unit(n, par, u):
                if u == 0:
                    pe.wait_ge(m_loaded, 16 * PARTS * (n + 1))
                pe.wait_ge(exp_done, n * UNITS + u + 1)
                for h, j, t0, w, c in P_UNITS[u]:
                    mm = pe.matmul(p_bank[u % 2][:, c:c + w], ks[:, par, j * P:(j + 1) * P],
                                   qs[:, par, h * T + t0:h * T + t0 + w], start=True, stop=True)
                mm.then_inc(p_full, 1)

            def pv(n, par, s):
                x = 0 if s < 3 else 1
                if s == 0:
                    pe.wait_ge(v_loaded, 16 * (n + 1))
                if s in (0, 3):
                    pe.wait_ge(o_copied, 2 * n + x + 1)
                pe.wait_ge(exp_done, n * UNITS + STEP_LAST_UNIT[s] + 1 + P_CREDIT)
                if HAS_DIAGONAL[s]:
                    pe.wait_ge(mask_done, n * MASKS + sum(HAS_DIAGONAL[:s + 1]))
                parts = STEP_PARTS[s]
                width = sum(w for _, _, w in parts)
                c = 0
                for j, t0, w in parts:
                    for h in range(HPG):
                        at = h * width + c
                        mm = pe.matmul(o_bank[x][32 * h:32 * (h + 1), t0 - 512 * x:t0 - 512 * x + w],
                                       vcur[:, par, j, :], pt[:, (par * STEPS + s) % 4, at:at + w],
                                       start=(s in (0, 3)), stop=(s in (2, STEPS - 1)), skip_group_check=True)
                    c += w
                mm.then_inc(pv_step, 1)

            def turn_outputs(m, r, n, x):
                dst = ring_fill(m, r)
                pe.wait_ge(o_copied, 2 * n + x + 1 + O_CREDIT)
                for i in range(4):
                    mm = pe.transpose(dst[:, P * i:P * (i + 1)], o_t[:, x, P * i:P * (i + 1)], ident)
                mm.then_inc(r_full, 1)

            def free_bank(m, c, kind):
                i = MOE_INDEX[c, kind]
                if i >= 2:
                    before, what = MOE_ITEMS[i - 2]
                    if what == "down":
                        pe.wait_ge(acc_added, m * CHUNKS + before + 1 + ACC_CREDIT)
                    else:
                        pe.wait_ge(factor_made, m * 2 * CHUNKS + up_count(before, int(what[2])))
                else:
                    pe.wait_ge(acc_added, m * CHUNKS + i - 1 + ACC_CREDIT)
                return m_bank[i % 2]

            def moe(m, par, items):
                for c, kind in items:
                    if kind != "down":
                        f = int(kind[2])
                        if c == 0 and f == 0:
                            pe.wait_ge(w_split, 4 * (m + 1))
                        dst = free_bank(m, c, kind)
                        tok = slice(CHUNK * c, CHUNK * (c + 1))
                        for i in range(2):
                            w = slice(DFF * i + P * f, DFF * i + P * (f + 1))
                            for a, (wt, xt) in enumerate(((w_h, xh), (w_h, xl), (w_l, xh))):
                                mm = pe.matmul(dst[:, CHUNK * i:CHUNK * (i + 1)], wt[:, par, w], xt[:, tok],
                                               start=(a == 0), stop=(a == 2))
                        mm.then_inc(up_made, 1)
                    else:
                        pe.wait_ge(h_made, m * 2 * CHUNKS + up_count(c, 1))
                        dst = free_bank(m, c, kind)
                        for i in range(2):
                            for f in range(2):
                                mm = pe.matmul(dst[:, D * i:D * (i + 1)], hh[:, c % 2, f, P * i:P * (i + 1)],
                                               w_down[:, par, D * f:D * (f + 1)], start=(f == 0), stop=(f == 1))
                        mm.then_inc(down_made, 1)

            def group(n, half, front):
                m = n + 1
                half_of[0] = 1 - half if front else 0
                r = 0
                for pos in range(POSITIONS):
                    if pos < UNITS:
                        prob_unit(n, half, pos)
                    if front:
                        for u in S_AT.get(pos, []):
                            score_unit(m, 1 - half, u, r)
                            r += 1
                        if pos == M_AT:
                            turn_maxima(m, r)
                            r += 1
                        moe(m, 1 - half, MOE_AT.get(pos, []))
                    else:
                        for what in TAIL_AT.get(pos, []):
                            tail(r, what)
                            r += 1
                    if pos in PV_AT:
                        pv(n, half, PV_AT[pos])
                    if pos in OT_AT:
                        turn_outputs(m, r, n, OT_AT[pos])
                        r += 1
                if not front:
                    for what in TAIL_END:
                        tail(r, what)
                        r += 1

            def tail(r, what):
                kind, b, i = what
                dst = ring_fill(NG, r)

                def taken(*w):
                    pe.wait_ge(r_free, NG * RING_PER_GROUP + TAIL_INDEX[w] + 1 + R_CREDIT)

                if kind == "turn" and b == 1:
                    taken("outputs", 1, i)
                if kind == "project":
                    taken("turn", b, i)
                for j in range(4):
                    part = dst[:, P * j:P * (j + 1)]
                    if kind == "comb":
                        mm = pe.transpose(part[0:E, :], comb[:, :, 4 * i + j], ident)
                    elif kind == "turn":
                        mm = pe.transpose(part, on[:, 4 * i + j, 2 * b:2 * b + 2, :].rearrange("p k c -> p (k c)"), ident)
                    else:
                        t = TB * b + 4 * i + j
                        pe.matmul(part, on_t[:, b, 4 * i + j, :], pkc("Wo"), start=True, stop=False)
                        mm = pe.matmul(part, comb_t[:, P * t:P * (t + 1)], pkc("b3", E), start=False, stop=True)
                mm.then_inc(r_full, 1)

            pe.sem_inc(pv_step, PT_CREDIT)
            pe.wait_ge(const_loaded, 16)
            for i in range(4):
                pe.wait_ge(xn_done, i // 2 + 1)
                for j in range(4):
                    mm = pe.transpose(bank[i][:, P * j:P * (j + 1)], xn[:, 4 * i + j, :], ident)
                mm.then_inc(xT_made, 1)
            pe.wait_ge(pack_loaded, 16)

            def q_of(b):
                for c in range(2):
                    if b == 0:
                        pe.wait_ge(xT_done, c + 1)
                    else:
                        pe.wait_ge(q_taken, c + 1)
                    tok = xT[:, T * b + 512 * c:T * b + 512 * (c + 1)]
                    pe.matmul(bank[4 + c][:, :], pkc("Wq"), tok, start=True, stop=True)
                    pe.matmul(bank[6 + c][:, :], pkc("Wqr"), tok, start=True, stop=True).then_inc(q_made, 1)

            q_of(0)
            pe.wait_ge(xT_done, 4)
            for i, w in ((0, "Wk"), (1, "Wkr")):
                for c in range(4):
                    mm = pe.matmul(bank[i][32 * c:32 * (c + 1), :], pkc(w), xT[:, 512 * c:512 * (c + 1)], start=True,
                                   stop=True)
            mm.then_inc(k_made, 1)
            for b in range(B):
                for j in range(TB):
                    t = TB * b + j
                    mm = pe.matmul(bank[2 + b][:, 40 * j:40 * (j + 1)], xT[:, P * t:P * (t + 1)], pkc("Wvg"),
                                   start=True, stop=True)
                mm.then_inc(vg_made, 1)
            q_of(1)

            pe.wait_ge(v_made, 2)
            pe.wait_ge(q_taken, 4)
            pe.wait_ge(xl_done, 4)
            pe.wait_ge(minus_loaded, 32)
            moe_at = _spread(0, UNITS - 1, len(MOE_ITEMS))
            for u in range(UNITS):
                score_unit(0, 0, u, u)
                moe(0, 0, [MOE_ITEMS[i] for i in moe_at.get(u, [])])
            turn_maxima(0, UNITS, RING_PER_GROUP - UNITS)
            pe.wait_ge(part_due, 1)

            with pe.Fori(0, NG // 2 - 1) as k:
                for half in range(2):
                    group(2 * k + half, half, True)
            group(NG - 2, 0, True)
            group(NG - 1, 1, False)


def _tables():
    import numpy as np

    c = np.zeros((P, CONST_N), np.float32)
    c[:, slice(*CONST["ident"])] = np.eye(P, dtype=np.float32)
    freq = np.exp(-(np.arange(0, DH, 2, dtype=np.float32) / np.float32(DH)) * np.log(np.float32(10000.0)))
    angle = np.arange(T, dtype=np.float32)[:, None] * freq.astype(np.float32)
    cos = np.repeat(np.cos(angle), 2, axis=1).T
    sin = np.repeat(np.sin(angle), 2, axis=1).T * np.tile(np.array([-1, 1], np.float32), DH // 2)[:, None]
    scale = np.float32(1) / np.sqrt(np.float32(DH))
    c[:, slice(*CONST["cosq"])] = np.tile(cos, (HEADS, 1)) * scale
    c[:, slice(*CONST["sinq"])] = np.tile(sin, (HEADS, 1)) * scale
    for name, t in (("cosk", cos), ("sink", sin)):
        halves = [np.tile(t[:, 512 * (i % 2):512 * (i % 2) + 512], (GROUPS, 1)) for i in range(4)]
        c[:, slice(*CONST[name])] = np.concatenate(halves)
    c[:, slice(*CONST["prio"])] = np.arange(E, 0, -1)
    key, query = np.meshgrid(np.arange(P), np.arange(P))
    mask = np.zeros((P, 512), np.float32)
    mask[:, 384:] = np.where(key > query, np.float32(MASKED), np.float32(0))
    c[:, slice(*CONST["mask"])] = mask
    return c


def kernel(**inputs):
    import ml_dtypes
    import numpy as np
    import concourse.bacc as _bacc
    from concourse import mybir as _mybir
    from concourse.bass_utils import run_bass_kernel_spmd as _run

    a = {k.replace("L0_attn_", "").replace("L0_ffn_", ""): np.asarray(v) for k, v in inputs.items()}
    swap = np.arange(D) ^ 1
    pack = np.zeros((P, PACK_N), np.float32)
    wide = {"Wq": a["Wq"], "Wqr": a["Wq"][:, swap], "Wk": a["Wk"], "Wkr": a["Wk"][:, swap[:32]],
            "Wvg": np.concatenate([a["Wv"], a["Wg"].T], axis=1), "bq": a["bq"][:, None], "bqr": a["bq"][swap][:, None],
            "bk": np.tile(a["bk"], 4)[:, None], "bkr": np.tile(a["bk"][swap[:32]], 4)[:, None],
            "bv": np.tile(a["bv"][None], (P, 1)), "Wo": a["Wo"], "bo": np.tile(a["bo"][None], (P, 1))}
    for name, w in wide.items():
        pack[:, slice(*PACK[name])] = w
    pack[0:E, slice(*PACK["b3"])] = a["b3"]
    wa = np.concatenate([a["W1"].transpose(0, 2, 1), a["W2"].transpose(0, 2, 1),
                         a["b1"].reshape(E, 2, P).transpose(0, 2, 1), a["b2"].reshape(E, 2, P).transpose(0, 2, 1)],
                        axis=2)
    wd = a["W3"].transpose(0, 2, 1).reshape(E, 2, P, D).transpose(0, 2, 1, 3).reshape(E, P, 2 * D)
    rows = np.zeros((2 * PARTS, HPG * T), ml_dtypes.bfloat16)
    rows[PARTS:] = -1
    arrays = {"x": a["x"], "pack": pack, "const": _tables(), "wa": wa, "wd": wd, "rows": rows}
    arrays = {f"in_{k}": np.ascontiguousarray(v) for k, v in arrays.items()}

    nc = _bacc.Bacc("TRN2", target_bir_lowering=False, num_devices=1)
    args = [nc.dram_tensor(n, v.shape, _mybir.dt.from_np(v.dtype), kind="ExternalInput").ap()
            for n, v in arrays.items()]
    args.append(nc.dram_tensor("out_x", (B, T, D), F32, kind="ExternalOutput").ap())
    attention_and_experts(nc, *args)
    return _run(nc, [arrays], core_ids=[0]).results[0]["out_x"]
```

```python
from contextlib import ExitStack

import concourse.bass as bass
from concourse import mybir

ALU = mybir.AluOpType
ACT = mybir.ActivationFunctionType
F32 = mybir.dt.float32
F32R = mybir.dt.float32r
BF16 = mybir.dt.bfloat16
AX_X = mybir.AxisListType.X

P = 128
B, T, D = 2, 1024, 128
HEADS, GROUPS, DH = 16, 4, 8
HPG = HEADS // GROUPS
E, DFF = 8, 256
TB = T // P
NTB = B * TB
NG = B * GROUPS
EPS = 1e-5
MASKED = -1e30
PARTS = 3
M_ROW = PARTS * PARTS * DH

PACK = {}
_at = 0
for _name, _n in (("Wq", 128), ("Wqr", 128), ("Wk", 32), ("Wkr", 32), ("Wvg", 40), ("bq", 1), ("bqr", 1), ("bk", 1),
                  ("bkr", 1), ("bv", 32), ("Wo", 128), ("bo", 128), ("b3", 128)):
    PACK[_name] = (_at, _at + _n)
    _at += _n
PACK_N = _at
CONST = {}
_at = 0
for _name, _n in (("ident", 128), ("cosk", 512), ("sink", 512), ("prio", 8), ("cosq", 1024), ("sinq", 1024),
                  ("mask", 512)):
    CONST[_name] = (_at, _at + _n)
    _at += _n
CONST_N = _at
CONST_FIRST = CONST["cosq"][0]

UNITS = 36
STEPS = 10
STEP_PARTS = [
    [(0, 0, 512)],
    [(1, 128, 384), (3, 384, 128)],
    [(2, 256, 256)],
    [(0, 512, 512)],
    [(1, 512, 512)],
    [(2, 512, 512)],
    [(3, 512, 512)],
    [(4, 512, 512)],
    [(5, 640, 384), (7, 896, 128)],
    [(6, 768, 256)],
]
P_UNITS = []
STEP_LAST_UNIT = []
STEP_OF_UNIT = []
for _s, _parts in enumerate(STEP_PARTS):
    if sum(p[2] for p in _parts) == 512:
        for _h in range(HPG):
            _c = 0
            _u = []
            for _j, _t0, _n in _parts:
                _u.append((_h, _j, _t0, _n, _c))
                _c += _n
            P_UNITS.append(_u)
            STEP_OF_UNIT.append(_s)
    else:
        _j, _t0, _n = _parts[0]
        for _h in (0, 2):
            P_UNITS.append([(_h, _j, _t0, _n, 0), (_h + 1, _j, _t0, _n, _n)])
            STEP_OF_UNIT.append(_s)
    STEP_LAST_UNIT.append(len(P_UNITS) - 1)
assert len(P_UNITS) == UNITS
HAS_DIAGONAL = [any(t0 == j * P for j, t0, n in parts) for parts in STEP_PARTS]
MASKS = sum(HAS_DIAGONAL)
S_UNITS = []
for _h in range(HPG):
    for _i in (3, 4, 5, 6, 7):
        S_UNITS.append([(_h, _i, 0, 512, 0)])
    S_UNITS.append([(_h, 7, 512, 512, 0)])
    S_UNITS.append([(_h, 0, 0, 128, 0), (_h, 2, 0, 384, 128)])
    S_UNITS.append([(_h, 4, 512, 128, 0), (_h, 6, 512, 384, 128)])
    S_UNITS.append([(_h, 1, 0, 256, 0), (_h, 5, 512, 256, 256)])
assert len(S_UNITS) == UNITS
RING_PER_GROUP = UNITS + 3
CHUNKS = 8
CHUNK = B * T // CHUNKS

POSITIONS = 40
PV_AT = {5: 0, 9: 1, 11: 2, 15: 3, 19: 4, 22: 5, 26: 6, 30: 7, 33: 8, 35: 9}
EVAC_AT = {12: 0, 36: 1}
OT_AT = {14: 0, 38: 1}
M_AT = 33
MOE_ITEMS = []
for _c in range(CHUNKS):
    MOE_ITEMS += [(_c, "up0"), (_c, "up1")] + ([(_c - 1, "down")] if _c else [])
MOE_ITEMS.append((CHUNKS - 1, "down"))
MOE_INDEX = {_item: _i for _i, _item in enumerate(MOE_ITEMS)}


def _spread(first, last, n):
    at = {}
    span = last - first + 1
    for i in range(n):
        at.setdefault(first + i * span // n, []).append(i)
    return at


S_AT = _spread(3, 31, UNITS)
P_AT = _spread(0, 33, UNITS)
MOE_AT = {}
for _i, _item in enumerate(MOE_ITEMS):
    MOE_AT.setdefault(min((_i * 8 + 2) // 5, 36) if _i < 23 else 38, []).append(_item)
H_LATER = 1


FIRST_SPAN = UNITS + 8
FIRST_MOE_AT = {_p: [MOE_ITEMS[_i] for _i in _which] for _p, _which in _spread(0, FIRST_SPAN - 2, len(MOE_ITEMS)).items()}
FIRST_TURN_AT = UNITS + 1
FIRST_UP_LATER, FIRST_DOWN_LATER = 1, 1
Q1_MAKE_AT = (0, 8)
Q1_ROPE_AT = (3, 10)
Q1_PART_AT = (13, 17, 21)


def up_count(c, f):
    return 2 * c + f + 1


TAIL_AT = {0: [("comb", 0, 0)], 2: [("comb", 0, 1)], 4: [("comb", 0, 2)], 6: [("comb", 0, 3)], 8: [("turn", 0, 0)],
           10: [("turn", 0, 1)], 12: [("project", 0, 0)], 14: [("project", 0, 1)], 20: [("turn", 1, 0)],
           23: [("project", 1, 0)]}
TAIL_END = [("turn", 1, 1), ("project", 1, 1)]
TAIL_INDEX = {}
_i = 0
for _p in range(POSITIONS):
    for _w in TAIL_AT.get(_p, []) + ([("outputs", 1, OT_AT[_p])] if _p in OT_AT else []):
        TAIL_INDEX[_w] = _i
        _i += 1
for _w in TAIL_END:
    TAIL_INDEX[_w] = _i
    _i += 1


def attention_and_experts(nc, x, pack, const, wa, wd, zrow, out):
    q_dram = nc.dram_tensor("q_parts", (NG, PARTS, DH, HPG * T), BF16).ap()
    k_dram = nc.dram_tensor("k_parts", (NG, PARTS, DH, T), BF16).ap()

    with ExitStack() as ctx:
        def sb(name, shape, dt=F32):
            return ctx.enter_context(nc.sbuf_tensor(name, shape, dt))

        def sem(name):
            return ctx.enter_context(nc.semaphore(name))

        pk = sb("pk", [P, PACK_N])
        cn = sb("cn", [P, CONST_N])
        xs = sb("xs", [P, NTB, D])
        junk = xs[:, :, :].rearrange("p (n i) c -> p n (i c)", n=4)
        acc = sb("acc", [P, NTB, D])
        stats = sb("stats", [P, NTB, 6])
        meanvar = sb("meanvar", [P, NTB, 2])
        rstd = sb("rstd", [P, NTB])
        deviation = sb("deviation", [P, NTB])
        xT = sb("xT", [P, B * T])
        xh = sb("xh", [P, B * T], F32R)
        xl = sb("xl", [P, B * T], F32R)
        q_part = sb("q_part", [P, PARTS, T], BF16)
        krope_a = sb("krope_a", [P, 512])
        krope_b = sb("krope_b", [P, 512])
        k_part = sb("k_part", [P, PARTS, 512], BF16)
        qs = sb("qs", [P, 2, HPG * T], BF16)
        ks = sb("ks", [P, 2, T], BF16)
        vt = sb("vt", [P, NG, TB, 32])
        vcur = sb("vcur", [P, 2, TB, 32])
        pt = sb("pt", [P, 4, HPG * 512])
        rope_a, rope_b = pt[:, 3, 0:T], pt[:, 3, T:2 * T]
        mx = sb("mx", [P, HPG, TB])
        mx_a = sb("mx_a", [P, HPG, 4])
        mx_b = sb("mx_b", [P, HPG, 4])
        mrow = sb("mrow", [HPG * TB, PARTS, P], BF16)
        mres = sb("mres", [HPG * TB, 2, P])
        o_t = sb("o_t", [P, 2, 512])
        rl = sb("rl", [P, 2, 16])
        on = sb("on", [P, TB, NG // 2, 2 * HPG * DH])
        xn = sb("xn", [P, NTB, D])
        on_t = xn[:, :, :].rearrange("p (b i) c -> p b i c", b=B)
        gate = sb("gate", [P, NTB, E])
        gtmp = sb("gtmp", [P, 5, NTB, E])
        gcol = sb("gcol", [P, 6, NTB])
        comb = sb("comb", [P, E, NTB])
        comb_cur = sb("comb_cur", [P, 2, NTB])
        comb_t = sb("comb_t", [E, B * T])
        w_raw = sb("w_raw", [P, 2, 2 * DFF + 4])
        w_h = sb("w_h", [P, 2, 2 * DFF], F32R)
        w_l = sb("w_l", [P, 2, 2 * DFF], F32R)
        w_down = sb("w_down", [P, 2, 2 * D])
        half_b1 = sb("half_b1", [P, 2, 2])
        th = sb("th", [P, 2, 2, CHUNK])
        zz = sb("zz", [P, 2, 2, CHUNK])
        h_part = sb("h_part", [P, 2, CHUNK])
        hh = sb("hh", [P, 2, 2, CHUNK])
        bank = [ctx.enter_context(nc.psum_tensor(f"bank{i}", [P, 512], F32)) for i in range(8)]
        p_bank = bank[0:2]
        last_p_bank = bank[0:2] + bank[6:8]
        r_bank = bank[2:5]
        o_bank = bank[5]
        m_bank = [bank[6], bank[7], bank[5]]

        def pkc(name, rows=P):
            a, b = PACK[name]
            return pk[0:rows, a:b]

        def cnc(name):
            a, b = CONST[name]
            return cn[:, a:b]

        ident = cnc("ident")

        x_loaded = [sem(f"x_loaded{b}") for b in range(B)]
        pack_loaded = sem("pack_loaded")
        const_loaded = sem("const_loaded")
        tables_loaded = sem("tables_loaded")
        var_due = sem("var_due")
        deviation_done = sem("deviation_done")
        xn_done = sem("xn_done")
        xT_made = sem("xT_made")
        xT_done = sem("xT_done")
        xh_done = sem("xh_done")
        xl_done = sem("xl_done")
        q_made = sem("q_made")
        q_taken = sem("q_taken")
        k_made = sem("k_made")
        k_taken = sem("k_taken")
        vg_made = sem("vg_made")
        part_due = sem("part_due")
        part_done = sem("part_done")
        q_stored = [sem(f"q_stored{b}") for b in range(B)]
        q_first = sem("q_first")
        k_stored = [sem(f"k_stored{b}") for b in range(B)]
        gate_due = sem("gate_due")
        gate_exp = sem("gate_exp")
        v_made = sem("v_made")
        comb_done = sem("comb_done")
        acc_begun = sem("acc_begun")
        cleared = sem("cleared")
        own = sem("own")
        stack_loaded = sem("stack_loaded")
        v_loaded = sem("v_loaded")
        w_loaded = [sem(f"w_loaded{par}") for par in range(2)]
        w_split = sem("w_split")
        comb_copied = sem("comb_copied")
        m_loaded = sem("m_loaded")
        minus_loaded = sem("minus_loaded")
        p_full = sem("p_full")
        exp_done = sem("exp_done")
        mask_done = sem("mask_done")
        pv_step = sem("pv_step")
        o_copied = sem("o_copied")
        r_full = sem("r_full")
        r_free = sem("r_free")
        mx_done = sem("mx_done")
        mrow_done = sem("mrow_done")
        up_made = sem("up_made")
        act_made = sem("act_made")
        factor_made = sem("factor_made")
        h_begun = sem("h_begun")
        h_made = sem("h_made")
        down_made = sem("down_made")
        acc_added = sem("acc_added")
        stored = sem("stored")
        P_CREDIT, R_CREDIT, PT_CREDIT, O_CREDIT, ACC_CREDIT = 2, 3, 4, 1, 2

        waited = sem("waited")
        STACK_DMAS = PARTS + 1 + 1
        PART_BASE = {"q0": 0, "k": 2 * PARTS, "q1": 3 * PARTS}

        block = ctx.enter_context(nc.Block())

        def wait_apart(eng, semaphore, value):
            eng.wait_ge(semaphore, value)
            eng.sem_inc(waited, 1)

        @block.sync
        def _(sp):
            def load_stack(m, par):
                for a in range(PARTS):
                    r = a * PARTS * DH
                    sp.dma_start(qs[r:r + PARTS * DH, par, :],
                                 q_dram[bass.ds(m, 1), a].to_broadcast([PARTS, DH, HPG * T])).then_inc(stack_loaded, 16)
                sp.dma_start(ks[0:M_ROW, par, :],
                             k_dram[bass.ds(m, 1)].rearrange("o a d t -> o (a d) t")
                             .to_broadcast([PARTS, PARTS * DH, T])).then_inc(stack_loaded, 16)
                sp.dma_start(qs[M_ROW:M_ROW + PARTS, par, :], zrow[0:PARTS, :]).then_inc(stack_loaded, 16)

            def load_v(m, par):
                sp.dma_start(vcur[:, par].rearrange("p j c -> p (j c)"),
                             vt[:, bass.ds(m, 1)].rearrange("p o j c -> p (o j c)")).then_inc(v_loaded, 16)

            def load_expert(m, par):
                sp.dma_start(w_raw[:, par, :], wa[bass.ds(m, 1)].rearrange("o p c -> (o p) c")).then_inc(w_loaded[par], 16)
                sp.dma_start(w_down[:, par, :], wd[bass.ds(m, 1)].rearrange("o p c -> (o p) c")).then_inc(w_loaded[par], 16)

            def load_maxima(m, par):
                sp.wait_ge(mrow_done, m + 1)
                for c in range(PARTS):
                    sp.dma_start(qs[M_ROW + c:M_ROW + c + 1, par, :], mrow[:, c, :]).then_inc(m_loaded, 16)

            def group(n, half, experts):
                sp.wait_ge(exp_done, n * UNITS + P_CREDIT)
                load_stack(n + 1, 1 - half)
                sp.wait_ge(pv_step, n * STEPS + PT_CREDIT)
                load_v(n + 1, 1 - half)
                if experts:
                    sp.wait_ge(acc_added, n * CHUNKS + CHUNKS + ACC_CREDIT)
                    load_expert(n + 2, half)
                load_maxima(n + 1, 1 - half)

            for b in range(B):
                sp.dma_start(xs[:, b * TB:(b + 1) * TB, :], x[b].rearrange("(i p) c -> p i c", p=P))\
                    .then_inc(x_loaded[b], 16)
            sp.dma_start(pk[:, :], pack).then_inc(pack_loaded, 16)
            for e in range(2):
                load_expert(e, e)
            sp.wait_ge(cleared, 2)
            for par in range(2):
                sp.dma_start(ks[M_ROW:M_ROW + PARTS, par, :], zrow[PARTS:2 * PARTS, 0:T]).then_inc(minus_loaded, 16)
            def store_q(b, g):
                for a in range(PARTS):
                    dst = q_dram[GROUPS * b + g, a].rearrange("d (h t) -> h d t", h=HPG)
                    sp.dma_start(dst, q_part[32 * g:32 * (g + 1), a, :]).then_inc(q_first if b + g == 0 else q_stored[b], 16)

            def store_k(b):
                for a in range(PARTS):
                    for half in range(2):
                        c = 2 * b + half
                        dst = k_dram[GROUPS * b:GROUPS * (b + 1), a, :, half * 512:(half + 1) * 512]
                        sp.dma_start(dst, k_part[32 * c:32 * (c + 1), a, :]).then_inc(k_stored[b], 16)

            sp.wait_ge(part_done, PART_BASE["q0"] + 2 * PARTS)
            store_q(0, 0)
            sp.wait_ge(part_done, PART_BASE["k"] + PARTS)
            store_k(0)
            sp.wait_ge(q_first, 16 * PARTS)
            sp.wait_ge(k_stored[0], 16 * 2 * PARTS)
            load_stack(0, 0)
            for g in range(1, GROUPS):
                store_q(0, g)
            store_k(1)
            sp.wait_ge(v_made, 2)
            load_v(0, 0)
            sp.wait_ge(q_stored[0], 16 * (GROUPS - 1) * PARTS)
            sp.wait_ge(k_stored[1], 16 * 2 * PARTS)
            sp.wait_ge(part_done, PART_BASE["q1"] + 2 * PARTS)
            for g in range(GROUPS):
                store_q(1, g)
            sp.wait_ge(q_stored[1], 16 * GROUPS * PARTS)
            load_maxima(0, 0)
            with sp.Fori(0, NG // 2 - 1) as k:
                for half in range(2):
                    group(2 * k + half, half, True)
            group(NG - 2, 0, False)
            for b in range(B):
                for i in range(2):
                    sp.wait_ge(r_free, NG * RING_PER_GROUP + TAIL_INDEX["project", b, i] + 1 + R_CREDIT)
                    sp.dma_start(out[b, 512 * i:512 * (i + 1)].rearrange("(i p) c -> p i c", p=P),
                                 acc[:, TB * b + 4 * i:TB * b + 4 * i + 4, :]).then_inc(stored, 16)
            sp.wait_ge(stored, 16 * B * 2)

        @block.gpsimd
        def _(pool):
            def split_expert(m, par, turn):
                wait_apart(pool, w_loaded[par], 32 * (turn + 1))
                pool.tensor_copy(w_h[:, par, :], w_raw[:, par, 0:2 * DFF]).then_inc(w_split, 1)
                pool.tensor_scalar(half_b1[:, par, :], w_raw[:, par, 2 * DFF:2 * DFF + 2], 0.5, None, ALU.mult)\
                    .then_inc(w_split, 1)
                pool.wait_ge(w_split, 3 * m + 1)
                pool.tensor_tensor(w_l[:, par, :], w_raw[:, par, 0:2 * DFF], w_h[:, par, :].bitcast(F32),
                                   ALU.subtract).then_inc(w_split, 1)

            def tokens_weights(m, par):
                pool.tensor_copy(comb_cur[:, par, :], comb[:, bass.ds(m, 1), :].rearrange("p o i -> p (o i)"))\
                    .then_inc(comb_copied, 1)

            def mask(n, half, s):
                wait_apart(pool, exp_done, n * UNITS + STEP_LAST_UNIT[s] + 1 + P_CREDIT)
                width = sum(w for _, _, w in STEP_PARTS[s])
                c = 0
                for _, _, w in STEP_PARTS[s]:
                    v = pt[:, (half * STEPS + s) % 4, 0:HPG * width].rearrange("p (h c) -> p h c", h=HPG)[:, :, c:c + P]
                    ins = pool.affine_select(out=v, in_=v, compare_op=ALU.is_ge, fill=0.0, base=0,
                                             pattern=[[0, HPG], [1, P]], channel_multiplier=-1)
                    c += w
                ins.then_inc(mask_done, 1)

            def expert_h(m, c, f):
                h = hh[:, c % 2, f, :]
                pool.wait_ge(factor_made, m * 2 * CHUNKS + up_count(c, f))
                pool.tensor_tensor(h_part[:, f, :], th[:, c % 2, f, :], h, ALU.mult).then_inc(h_begun, 1)
                pool.wait_ge(h_begun, m * 2 * CHUNKS + up_count(c, f))
                pool.tensor_tensor(h, h_part[:, f, :], h, ALU.add).then_inc(h_made, 1)

            def group(n, half, front, k=None):
                for pos in range(POSITIONS):
                    for s in range(STEPS):
                        if STEP_LAST_UNIT[s] in P_AT.get(pos, []) and HAS_DIAGONAL[s]:
                            mask(n, half, s)
                    if front:
                        for c, kind in MOE_AT.get(pos - H_LATER, []):
                            if kind != "down":
                                expert_h(n + 1, c, int(kind[2]))
                    if k is not None and pos == 12:
                        split_expert(n + 2, half, k + 1)
                        tokens_weights(n + 2, half)
                if front:
                    for pos in range(POSITIONS - H_LATER, POSITIONS):
                        assert all(kind == "down" for c, kind in MOE_AT.get(pos, []))

            pool.memset(qs[:, :, :].bitcast(F32), 0.0).then_inc(cleared, 1)
            pool.memset(ks[:, :, :].bitcast(F32), 0.0).then_inc(cleared, 1)
            pool.memset(vt[:, :, :, :], 0.0).then_inc(cleared, 1)
            pool.wait_ge(cleared, 3)
            pool.memset(vt[:, :, :, DH:DH + 1], 1.0).then_inc(cleared, 1)
            for b in range(B):
                pool.wait_ge(x_loaded[b], 16)
            pool.wait_ge(pack_loaded, 16)
            pool.tensor_tensor(acc[:, :, :], xs[:, :, :], pkc("bo").unsqueeze(1).to_broadcast([P, NTB, D]), ALU.add)\
                .then_inc(acc_begun, 1)
            for i in range(4):
                pool.wait_ge(xh_done, i + 1)
                pool.tensor_tensor(xl[:, 512 * i:512 * (i + 1)], xT[:, 512 * i:512 * (i + 1)],
                                   xh[:, 512 * i:512 * (i + 1)].bitcast(F32), ALU.subtract).then_inc(xl_done, 1)
            for e in range(2):
                split_expert(e, e, 0)
            pool.wait_ge(comb_done, 1)
            for e in range(2):
                tokens_weights(e, e)
            for c in range(CHUNKS):
                for f in range(2):
                    expert_h(0, c, f)
            with pool.Fori(0, NG // 2 - 1) as k:
                for half in range(2):
                    group(2 * k + half, half, True, k)
            group(NG - 2, 0, True)
            group(NG - 1, 1, False)

        @block.scalar
        def _(act):
            def exp_unit(n, half, u, banks):
                s = STEP_OF_UNIT[u]
                first = STEP_LAST_UNIT[s - 1] + 1 if s else 0
                if u == first:
                    act.wait_ge(pv_step, n * STEPS + s + 1)
                act.wait_ge(p_full, n * UNITS + u + 1)
                at = (u - first) * 512
                nc.scalar.activation(pt[:, (half * STEPS + s) % 4, at:at + 512], banks[u % len(banks)][:, :], ACT.Exp)\
                    .then_inc(exp_done, 1)

            def expert_act(m, par, c, f, banks=2):
                act.wait_ge(up_made, m * 2 * CHUNKS + 2 * c + f + 1)
                src = m_bank[MOE_INDEX[c, f"up{f}"] % banks][:, 0:CHUNK]
                nc.scalar.activation(th[:, c % 2, f, :], src, ACT.Tanh, bias=half_b1[:, par, f:f + 1], scale=0.5)
                nc.scalar.activation(zz[:, c % 2, f, :], src, ACT.Identity, bias=half_b1[:, par, f:f + 1], scale=0.5)\
                    .then_inc(act_made, 1)

            def copy_outputs(n, x):
                act.wait_ge(pv_step, n * STEPS + (3, STEPS)[x] + PT_CREDIT)
                nc.scalar.copy(o_t[:, x, :], o_bank[:, :]).then_inc(o_copied, 1)

            def group(n, half, front):
                for pos in range(POSITIONS):
                    for u in P_AT.get(pos, []):
                        exp_unit(n, half, u, p_bank if front else last_p_bank)
                    if front:
                        for c, kind in MOE_AT.get(pos, []):
                            if kind != "down":
                                expert_act(n + 1, 1 - half, c, int(kind[2]))
                    if pos in EVAC_AT:
                        copy_outputs(n, EVAC_AT[pos])

            act.dma_start(cn[:, 0:CONST_FIRST], const[:, 0:CONST_FIRST]).then_inc(const_loaded, 16)
            act.dma_start(cn[:, CONST_FIRST:CONST_N], const[:, CONST_FIRST:CONST_N]).then_inc(tables_loaded, 16)
            act.sem_inc(exp_done, P_CREDIT)
            act.sem_inc(o_copied, O_CREDIT)
            for b in range(B):
                act.wait_ge(var_due, b + 1)
                nc.scalar.activation(deviation[:, TB * b:TB * (b + 1)], rstd[:, TB * b:TB * (b + 1)], ACT.Sqrt)\
                    .then_inc(deviation_done, 1)
            for i in range(4):
                act.wait_ge(xT_made, i + 1)
                nc.scalar.copy(xT[:, 512 * i:512 * (i + 1)], bank[i][:, :]).then_inc(xT_done, 1)
            for i in range(4):
                nc.scalar.copy(xh[:, 512 * i:512 * (i + 1)], bank[i][:, :]).then_inc(xh_done, 1)

            def round_q(b, a):
                for c in range(2):
                    act.wait_ge(part_due, PART_BASE[f"q{b}"] + 2 * a + c + 1)
                    half = slice(512 * c, 512 * (c + 1))
                    nc.scalar.copy(q_part[:, a, half], rope_a[:, half]).then_inc(part_done, 1)

            for a in range(PARTS):
                round_q(0, a)
            for a in range(PARTS):
                act.wait_ge(part_due, PART_BASE["k"] + a + 1)
                nc.scalar.copy(k_part[:, a, :], krope_a[:, :]).then_inc(part_done, 1)
            act.wait_ge(gate_due, 1)
            nc.scalar.activation(gcol[:, 3, :], gcol[:, 2, :], ACT.Exp).then_inc(gate_exp, 1)
            for u in range(FIRST_SPAN):
                for c, kind in FIRST_MOE_AT.get(u, []):
                    if kind != "down":
                        expert_act(0, 0, c, int(kind[2]), 3)
                if u - 1 in Q1_PART_AT:
                    a = Q1_PART_AT.index(u - 1)
                    if a == 0:
                        act.wait_ge(q_first, 16 * PARTS)
                        act.wait_ge(q_stored[0], 16 * (GROUPS - 1) * PARTS)
                    round_q(1, a)
            with act.Fori(0, NG // 2 - 1) as k:
                for half in range(2):
                    group(2 * k + half, half, True)
            group(NG - 2, 0, True)
            group(NG - 1, 1, False)

        @block.vector
        def _(dve):
            steps = [0]

            def link(ins):
                ins.then_inc(own, 1)
                steps[0] += 1
                dve.wait_ge(own, steps[0])

            ring = {}

            def score_unit(m, u, r):
                wait_apart(dve, r_full, m_ring(m) + r + 1)
                b = r_bank[r % len(r_bank)]
                for h, i, s0, w, c in S_UNITS[u]:
                    src = b[:, c:c + w]
                    if i < 4:
                        dst = mx[:, h, i:i + 1]
                    else:
                        dst = (mx_b if s0 else mx_a)[:, h, i - 4:i - 3]
                    if s0 + w == (i + 1) * P:
                        ins = dve.tensor_tensor_reduce(junk[:, r % len(r_bank), c:c + w], src, cnc("mask")[:, 512 - w:512],
                                                       1.0, MASKED, ALU.add, ALU.max, dst)
                    else:
                        ins = dve.tensor_reduce(dst, src, AX_X, ALU.max)
                ins.then_inc(r_free, 1)

            def m_ring(m):
                return m * RING_PER_GROUP

            def group_maxima(m):
                dve.wait_ge(r_free, m_ring(m) + ring["last_score"] + 1 + R_CREDIT)
                dve.tensor_tensor(mx[:, :, 4:8], mx_a[:, :, :], mx_b[:, :, :], ALU.max).then_inc(mx_done, 1)

            def maxima_rows(m, r, taken=1):
                dve.wait_ge(r_full, m_ring(m) + r + 1)
                src = r_bank[r % len(r_bank)][0:HPG * TB, 0:P]
                base = 3 * m
                dve.tensor_copy(mrow[:, 0, :], src).then_inc(mstep, 1)
                dve.wait_ge(mstep, base + 1)
                dve.tensor_tensor(mres[:, 0, :], src, mrow[:, 0, :], ALU.subtract).then_inc(r_free, taken)
                dve.wait_ge(r_free, m_ring(m) + r + taken + R_CREDIT)
                dve.tensor_copy(mrow[:, 1, :], mres[:, 0, :]).then_inc(mstep, 1)
                dve.wait_ge(mstep, base + 2)
                dve.tensor_tensor(mres[:, 1, :], mres[:, 0, :], mrow[:, 1, :], ALU.subtract).then_inc(mstep, 1)
                dve.wait_ge(mstep, base + 3)
                dve.tensor_copy(mrow[:, 2, :], mres[:, 1, :]).then_inc(mrow_done, 1)

            mstep = sem("mstep")
            rlstep = sem("rlstep")

            def outputs(m, r, n, k, half, x):
                dve.wait_ge(r_full, m_ring(m) + r + 1)
                src = r_bank[r % len(r_bank)][:, :].rearrange("p (i h c) -> p i h c", i=4, h=HPG)
                flat = r_bank[r % len(r_bank)][:, :].rearrange("p (q c) -> p q c", c=32)
                dve.reciprocal(rl[:, x, :], flat[:, :, DH]).then_inc(rlstep, 1)
                dve.wait_ge(rlstep, 2 * n + x + 1)
                dst = on[:, 4 * x:4 * x + 4, bass.ds(k, 1), 32 * half:32 * half + 32]
                dst = dst.rearrange("p i o (h d) -> p (i o) h d", h=HPG)
                inv = rl[:, x, :].rearrange("p (i h) -> p i h", i=4).unsqueeze(3).to_broadcast([P, 4, HPG, DH])
                dve.tensor_tensor(dst, src[:, :, :, 0:DH], inv, ALU.mult).then_inc(r_free, 1)

            def expert_factor(m, par, c, f, banks):
                dve.wait_ge(act_made, m * 2 * CHUNKS + up_count(c, f))
                dve.scalar_tensor_tensor(out=hh[:, c % 2, f, :],
                                         in0=m_bank[MOE_INDEX[c, f"up{f}"] % banks][:, CHUNK:2 * CHUNK],
                                         scalar=w_raw[:, par, 2 * DFF + 2 + f:2 * DFF + 3 + f], in1=zz[:, c % 2, f, :],
                                         op0=ALU.add, op1=ALU.mult).then_inc(factor_made, 1)

            def expert_add(m, par, c, banks):
                if c == 0:
                    dve.wait_ge(comb_copied, m + 1)
                dve.wait_ge(down_made, m * CHUNKS + c + 1)
                for i in range(2):
                    t = 2 * c + i
                    ins = dve.scalar_tensor_tensor(out=acc[:, t, :], in0=m_bank[MOE_INDEX[c, "down"] % banks][:, D * i:D * (i + 1)],
                                                   scalar=comb_cur[:, par, t:t + 1], in1=acc[:, t, :],
                                                   op0=ALU.mult, op1=ALU.add)
                ins.then_inc(acc_added, 1)

            def moe(m, par, items, banks=2):
                for c, kind in items:
                    if kind == "down":
                        expert_add(m, par, c, banks)
                    else:
                        expert_factor(m, par, c, int(kind[2]), banks)

            def due(pos):
                return ([w for w in MOE_AT.get(pos - 2, []) if w[1] != "down"]
                        + [w for w in MOE_AT.get(pos - 1, []) if w[1] == "down"])

            def group(n, k, half, front):
                m = n + 1
                r = 0
                for pos in range(POSITIONS):
                    if front:
                        moe(m, 1 - half, due(pos))
                    if front:
                        for u in S_AT.get(pos, []):
                            score_unit(m, u, r)
                            ring["last_score"] = r
                            r += 1
                        if pos == M_AT - 1:
                            group_maxima(m)
                        if pos == M_AT:
                            maxima_rows(m, r)
                            r += 1
                    if pos in OT_AT:
                        outputs(m, r, n, k, half, OT_AT[pos])
                        r += 1
                if front:
                    for pos in (POSITIONS, POSITIONS + 1):
                        moe(m, 1 - half, due(pos))

            dve.sem_inc(r_free, R_CREDIT)
            dve.sem_inc(acc_added, ACC_CREDIT)
            for b in range(B):
                lo, hi = b * TB, (b + 1) * TB
                dve.wait_ge(x_loaded[b], 16)
                for i in range(lo, hi):
                    ins = dve.bn_stats(stats[:, i, :], xs[:, i, :])
                link(ins)
                for i in range(lo, hi):
                    ins = dve.bn_aggr(meanvar[:, i, :], stats[:, i, :])
                link(ins)
                dve.tensor_scalar(rstd[:, lo:hi], meanvar[:, lo:hi, 1], EPS, None, ALU.add).then_inc(var_due, 1)
                dve.wait_ge(deviation_done, b + 1)
                link(dve.reciprocal(rstd[:, lo:hi], deviation[:, lo:hi]))
                for i in range(lo, hi):
                    ins = dve.tensor_scalar(xn[:, i, :], xs[:, i, :], meanvar[:, i, 0:1], rstd[:, i:i + 1],
                                            ALU.subtract, ALU.mult)
                ins.then_inc(xn_done, 1)
            dve.wait_ge(pack_loaded, 16)
            dve.wait_ge(const_loaded, 16)

            def rope(dst_a, dst_b, made, at, bank_q, bank_r, bias, bias_r, cos, sin):
                dve.wait_ge(made, at)
                dve.scalar_tensor_tensor(out=dst_a, in0=bank_q[:, :], scalar=pkc(bias), in1=cos, op0=ALU.add,
                                         op1=ALU.mult)
                return dve.scalar_tensor_tensor(out=dst_b, in0=bank_r[:, :], scalar=pkc(bias_r), in1=sin,
                                                op0=ALU.add, op1=ALU.mult)

            def rope_q(b, c, bank_q, bank_r):
                half = slice(512 * c, 512 * (c + 1))
                rope(rope_a[:, half], rope_b[:, half], q_made, 2 * b + c + 1, bank_q, bank_r, "bq", "bqr",
                     cnc("cosq")[:, half], cnc("sinq")[:, half]).then_inc(q_taken, 1)

            def part_q(b, a):
                for c in range(2):
                    half = slice(512 * c, 512 * (c + 1))
                    if a == 0:
                        dve.wait_ge(q_taken, 2 * b + c + 1)
                        other = rope_b[:, half]
                    else:
                        dve.wait_ge(part_done, PART_BASE[f"q{b}"] + 2 * (a - 1) + c + 1)
                        other = q_part[:, a - 1, half]
                    dve.tensor_tensor(rope_a[:, half], rope_a[:, half], other, ALU.subtract if a else ALU.add)\
                        .then_inc(part_due, 1)

            dve.wait_ge(tables_loaded, 16)
            for c in range(2):
                rope_q(0, c, bank[4 + c], bank[6 + c])
            for a in range(PARTS):
                part_q(0, a)
            rope(krope_a[:, :], krope_b[:, :], k_made, 1, bank[0], bank[1], "bk", "bkr", cnc("cosk"), cnc("sink"))\
                .then_inc(k_taken, 1)
            dve.wait_ge(k_taken, 1)
            dve.tensor_tensor(krope_a[:, :], krope_a[:, :], krope_b[:, :], ALU.add).then_inc(part_due, 1)
            for a in range(PARTS - 1):
                dve.wait_ge(part_done, PART_BASE["k"] + a + 1)
                dve.tensor_tensor(krope_a[:, :], krope_a[:, :], k_part[:, a, :], ALU.subtract).then_inc(part_due, 1)
            for b in range(B):
                dve.wait_ge(vg_made, b + 1)
                if b == 0:
                    dve.wait_ge(cleared, 4)
                src = bank[2 + b][:, 0:TB * 40].rearrange("p (j c) -> p j c", c=40)
                for g in range(GROUPS):
                    ins = dve.tensor_tensor(vt[:, GROUPS * b + g, :, 0:DH], src[:, :, DH * g:DH * (g + 1)],
                                            pkc("bv")[:, DH * g:DH * (g + 1)].unsqueeze(1).to_broadcast([P, TB, DH]),
                                            ALU.add)
                dve.tensor_copy(gate[:, TB * b:TB * (b + 1), :], src[:, :, 32:40]).then_inc(v_made, 1)
            dve.wait_ge(v_made, 2)

            def col(i):
                return gcol[:, i, :].unsqueeze(2).to_broadcast([P, NTB, E])

            prio = cnc("prio").unsqueeze(1).to_broadcast([P, NTB, E])
            left = gate
            for i in range(2):
                best, eq, one = gcol[:, i, :], gtmp[:, 0], gtmp[:, 1 + i]
                link(dve.tensor_reduce(best, left[:, :, :], AX_X, ALU.max))
                link(dve.tensor_tensor(eq, left[:, :, :], col(i), ALU.is_equal))
                link(dve.tensor_tensor(eq, eq, prio, ALU.mult))
                link(dve.tensor_reduce(gcol[:, 4, :], eq, AX_X, ALU.max))
                link(dve.tensor_tensor(one, eq, col(4), ALU.is_equal))
                if i == 0:
                    link(dve.scalar_tensor_tensor(out=gtmp[:, 3], in0=one, scalar=-3e38, in1=gate[:, :, :],
                                                  op0=ALU.mult, op1=ALU.add))
                    left = gtmp[:, 3]
            dve.tensor_tensor(gcol[:, 2, :], gcol[:, 1, :], gcol[:, 0, :], ALU.subtract).then_inc(gate_due, 1)
            dve.wait_ge(gate_exp, 1)
            link(dve.tensor_scalar(gcol[:, 5, :], gcol[:, 3, :], 1.0, None, ALU.add))
            link(dve.reciprocal(gcol[:, 0, :], gcol[:, 5, :]))
            link(dve.tensor_tensor(gcol[:, 1, :], gcol[:, 3, :], gcol[:, 0, :], ALU.mult))
            dve.tensor_tensor(gtmp[:, 0], gtmp[:, 1], col(0), ALU.mult)
            link(dve.tensor_tensor(gtmp[:, 4], gtmp[:, 2], col(1), ALU.mult))
            dve.tensor_tensor(comb[:, :, :].rearrange("p e i -> p i e"), gtmp[:, 0], gtmp[:, 4], ALU.add)\
                .then_inc(comb_done, 1)
            dve.wait_ge(acc_begun, 1)

            dve.wait_ge(acc_begun, 1)

            def first_due(u):
                return ([w for w in FIRST_MOE_AT.get(u - FIRST_UP_LATER, []) if w[1] != "down"]
                        + [w for w in FIRST_MOE_AT.get(u - FIRST_DOWN_LATER, []) if w[1] == "down"])

            r = 0
            for u in range(UNITS):
                if u in Q1_ROPE_AT:
                    if u == Q1_ROPE_AT[0]:
                        dve.wait_ge(part_done, PART_BASE["q0"] + 2 * PARTS)
                    rope_q(1, Q1_ROPE_AT.index(u), bank[0], bank[1])
                if u in Q1_PART_AT:
                    part_q(1, Q1_PART_AT.index(u))
                moe(0, 0, first_due(u), 3)
                score_unit(0, u, r)
                ring["last_score"] = r
                r += 1
            for u in range(UNITS, FIRST_SPAN + FIRST_UP_LATER):
                if u == UNITS:
                    group_maxima(0)
                if u == FIRST_TURN_AT:
                    maxima_rows(0, r, RING_PER_GROUP - UNITS)
                moe(0, 0, first_due(u), 3)

            with dve.Fori(0, NG // 2 - 1) as k:
                for half in range(2):
                    group(2 * k + half, k, half, True)
            group(NG - 2, NG // 2 - 1, 0, True)

            def tail(r, what):
                kind, b, i = what
                dve.wait_ge(r_full, m_ring(NG) + r + 1)
                src = r_bank[r % len(r_bank)]
                if kind == "comb":
                    ins = dve.tensor_copy(comb_t[:, 512 * i:512 * (i + 1)], src[0:E, :])
                elif kind == "turn":
                    ins = dve.tensor_copy(on_t[:, b, 4 * i:4 * i + 4, :].rearrange("p i c -> p (i c)"), src[:, :])
                else:
                    dst = acc[:, TB * b + 4 * i:TB * b + 4 * i + 4, :].rearrange("p i c -> p (i c)")
                    ins = dve.tensor_tensor(dst, dst, src[:, :], ALU.add)
                ins.then_inc(r_free, 1)

            m = NG
            r = 0
            for pos in range(POSITIONS):
                for what in TAIL_AT.get(pos, []):
                    tail(r, what)
                    r += 1
                if pos in OT_AT:
                    outputs(m, r, NG - 1, NG // 2 - 1, 1, OT_AT[pos])
                    r += 1
            for what in TAIL_END:
                tail(r, what)
                r += 1

        @block.tensor
        def _(pe):
            def ring_fill(m, r):
                pe.wait_ge(r_free, m * RING_PER_GROUP + r + 1)
                return r_bank[r % len(r_bank)]

            def score_unit(m, par, u, r):
                if u == 0:
                    pe.wait_ge(stack_loaded, 16 * STACK_DMAS * (m + 1))
                dst = ring_fill(m, r)
                for h, i, s0, w, c in S_UNITS[u]:
                    q0 = h * T + i * P
                    mm = pe.matmul(dst[:, c:c + w], qs[:, par, q0:q0 + P], ks[:, par, s0:s0 + w], start=True,
                                   stop=True)
                mm.then_inc(r_full, 1)

            def turn_maxima(m, r, made=1):
                dst = ring_fill(m, r)
                pe.wait_ge(mx_done, m + 1)
                pe.transpose(dst[0:HPG * TB, 0:P], mx[:, :, :].rearrange("p h i -> p (h i)"), ident)\
                    .then_inc(r_full, made)

            def prob_unit(n, par, u, banks=p_bank):
                if u == 0:
                    pe.wait_ge(m_loaded, 16 * PARTS * (n + 1))
                ago = P_CREDIT if u < P_CREDIT else len(banks)
                pe.wait_ge(exp_done, n * UNITS + u - ago + 1 + P_CREDIT)
                for h, j, t0, w, c in P_UNITS[u]:
                    mm = pe.matmul(banks[u % len(banks)][:, c:c + w], ks[:, par, j * P:(j + 1) * P],
                                   qs[:, par, h * T + t0:h * T + t0 + w], start=True, stop=True)
                mm.then_inc(p_full, 1)

            def pv(n, par, s):
                x = 0 if s < 3 else 1
                if s == 0:
                    pe.wait_ge(v_loaded, 16 * (n + 1))
                if s in (0, 3):
                    pe.wait_ge(o_copied, 2 * n + x + 1)
                pe.wait_ge(exp_done, n * UNITS + STEP_LAST_UNIT[s] + 1 + P_CREDIT)
                if HAS_DIAGONAL[s]:
                    pe.wait_ge(mask_done, n * MASKS + sum(HAS_DIAGONAL[:s + 1]))
                parts = STEP_PARTS[s]
                width = sum(w for _, _, w in parts)
                c = 0
                for j, t0, w in parts:
                    for h in range(HPG):
                        at = h * width + c
                        mm = pe.matmul(o_bank[32 * h:32 * (h + 1), t0 - 512 * x:t0 - 512 * x + w],
                                       vcur[:, par, j, :], pt[:, (par * STEPS + s) % 4, at:at + w],
                                       start=(s in (0, 3)), stop=(s in (2, STEPS - 1)), skip_group_check=True)
                    c += w
                mm.then_inc(pv_step, 1)

            def turn_outputs(m, r, n, x):
                dst = ring_fill(m, r)
                pe.wait_ge(o_copied, 2 * n + x + 1 + O_CREDIT)
                for i in range(4):
                    mm = pe.transpose(dst[:, P * i:P * (i + 1)], o_t[:, x, P * i:P * (i + 1)], ident)
                mm.then_inc(r_full, 1)

            def free_bank(m, c, kind, banks):
                i = MOE_INDEX[c, kind]
                if i >= banks:
                    before, what = MOE_ITEMS[i - banks]
                    if what == "down":
                        pe.wait_ge(acc_added, m * CHUNKS + before + 1 + ACC_CREDIT)
                    else:
                        pe.wait_ge(factor_made, m * 2 * CHUNKS + up_count(before, int(what[2])))
                elif banks == 2:
                    pe.wait_ge(acc_added, m * CHUNKS + i - 1 + ACC_CREDIT)
                return m_bank[i % banks]

            def moe(m, par, items, banks=2):
                for c, kind in items:
                    if kind != "down":
                        f = int(kind[2])
                        if c == 0 and f == 0:
                            pe.wait_ge(w_split, 3 * (m + 1))
                        dst = free_bank(m, c, kind, banks)
                        tok = slice(CHUNK * c, CHUNK * (c + 1))
                        for i in range(2):
                            w = slice(DFF * i + P * f, DFF * i + P * (f + 1))
                            for a, (wt, xt) in enumerate(((w_h, xh), (w_h, xl), (w_l, xh))):
                                mm = pe.matmul(dst[:, CHUNK * i:CHUNK * (i + 1)], wt[:, par, w], xt[:, tok],
                                               start=(a == 0), stop=(a == 2))
                        mm.then_inc(up_made, 1)
                    else:
                        pe.wait_ge(h_made, m * 2 * CHUNKS + up_count(c, 1))
                        dst = free_bank(m, c, kind, banks)
                        for i in range(2):
                            for f in range(2):
                                mm = pe.matmul(dst[:, D * i:D * (i + 1)], hh[:, c % 2, f, P * i:P * (i + 1)],
                                               w_down[:, par, D * f:D * (f + 1)], start=(f == 0), stop=(f == 1))
                        mm.then_inc(down_made, 1)

            def group(n, half, front):
                m = n + 1
                r = 0
                for pos in range(POSITIONS):
                    for u in P_AT.get(pos, []):
                        prob_unit(n, half, u, p_bank if front else last_p_bank)
                    if front:
                        for u in S_AT.get(pos, []):
                            score_unit(m, 1 - half, u, r)
                            r += 1
                        if pos == M_AT:
                            turn_maxima(m, r)
                            r += 1
                        moe(m, 1 - half, MOE_AT.get(pos, []))
                    else:
                        for what in TAIL_AT.get(pos, []):
                            tail(r, what)
                            r += 1
                    if pos in PV_AT:
                        pv(n, half, PV_AT[pos])
                    if pos in OT_AT:
                        turn_outputs(m, r, n, OT_AT[pos])
                        r += 1
                if not front:
                    for what in TAIL_END:
                        tail(r, what)
                        r += 1

            def tail(r, what):
                kind, b, i = what
                dst = ring_fill(NG, r)

                def taken(*w):
                    pe.wait_ge(r_free, NG * RING_PER_GROUP + TAIL_INDEX[w] + 1 + R_CREDIT)

                if kind == "turn" and b == 1:
                    taken("outputs", 1, i)
                if kind == "project":
                    taken("turn", b, i)
                for j in range(4):
                    part = dst[:, P * j:P * (j + 1)]
                    if kind == "comb":
                        mm = pe.transpose(part[0:E, :], comb[:, :, 4 * i + j], ident)
                    elif kind == "turn":
                        mm = pe.transpose(part, on[:, 4 * i + j, 2 * b:2 * b + 2, :].rearrange("p k c -> p (k c)"), ident)
                    else:
                        t = TB * b + 4 * i + j
                        pe.matmul(part, on_t[:, b, 4 * i + j, :], pkc("Wo"), start=True, stop=False)
                        mm = pe.matmul(part, comb_t[:, P * t:P * (t + 1)], pkc("b3", E), start=False, stop=True)
                mm.then_inc(r_full, 1)

            pe.sem_inc(pv_step, PT_CREDIT)
            pe.wait_ge(const_loaded, 16)

            def turn_tokens(i):
                pe.wait_ge(xn_done, i // 2 + 1)
                for j in range(4):
                    mm = pe.transpose(bank[i][:, P * j:P * (j + 1)], xn[:, 4 * i + j, :], ident)
                mm.then_inc(xT_made, 1)

            def make_q(b, c, bank_q, bank_r):
                tok = xT[:, T * b + 512 * c:T * b + 512 * (c + 1)]
                pe.matmul(bank_q[:, :], pkc("Wq"), tok, start=True, stop=True)
                pe.matmul(bank_r[:, :], pkc("Wqr"), tok, start=True, stop=True).then_inc(q_made, 1)

            for i in range(2):
                turn_tokens(i)
            pe.wait_ge(pack_loaded, 16)
            for c in range(2):
                pe.wait_ge(xT_done, c + 1)
                make_q(0, c, bank[4 + c], bank[6 + c])
            for i in range(2, 4):
                turn_tokens(i)
            pe.wait_ge(xT_done, 4)
            pe.wait_ge(xh_done, 2)
            for i, w in ((0, "Wk"), (1, "Wkr")):
                for c in range(4):
                    mm = pe.matmul(bank[i][32 * c:32 * (c + 1), :], pkc(w), xT[:, 512 * c:512 * (c + 1)], start=True,
                                   stop=True)
            mm.then_inc(k_made, 1)
            pe.wait_ge(xh_done, 4)
            for b in range(B):
                for j in range(TB):
                    t = TB * b + j
                    mm = pe.matmul(bank[2 + b][:, 40 * j:40 * (j + 1)], xT[:, P * t:P * (t + 1)], pkc("Wvg"),
                                   start=True, stop=True)
                mm.then_inc(vg_made, 1)

            pe.wait_ge(q_taken, 2)
            pe.wait_ge(k_taken, 1)
            pe.wait_ge(v_made, 2)
            pe.wait_ge(xl_done, 4)
            for u in range(FIRST_SPAN):
                if u in Q1_MAKE_AT:
                    c = Q1_MAKE_AT.index(u)
                    if c:
                        pe.wait_ge(q_taken, 2 + c)
                    make_q(1, c, bank[0], bank[1])
                moe(0, 0, FIRST_MOE_AT.get(u, []), 3)
                if u == 0:
                    pe.wait_ge(minus_loaded, 32)
                if u < UNITS:
                    score_unit(0, 0, u, u)
                if u == FIRST_TURN_AT:
                    turn_maxima(0, UNITS, RING_PER_GROUP - UNITS)
            pe.wait_ge(q_taken, 4)
            pe.wait_ge(acc_added, CHUNKS + ACC_CREDIT)

            with pe.Fori(0, NG // 2 - 1) as k:
                for half in range(2):
                    group(2 * k + half, half, True)
            group(NG - 2, 0, True)
            pe.wait_ge(acc_added, NG * CHUNKS + ACC_CREDIT)
            group(NG - 1, 1, False)


def _tables():
    import numpy as np

    c = np.zeros((P, CONST_N), np.float32)
    c[:, slice(*CONST["ident"])] = np.eye(P, dtype=np.float32)
    freq = np.exp(-(np.arange(0, DH, 2, dtype=np.float32) / np.float32(DH)) * np.log(np.float32(10000.0)))
    angle = np.arange(T, dtype=np.float32)[:, None] * freq.astype(np.float32)
    cos = np.repeat(np.cos(angle), 2, axis=1).T
    sin = np.repeat(np.sin(angle), 2, axis=1).T * np.tile(np.array([-1, 1], np.float32), DH // 2)[:, None]
    scale = np.float32(1) / np.sqrt(np.float32(DH))
    c[:, slice(*CONST["cosq"])] = np.tile(cos, (HEADS, 1)) * scale
    c[:, slice(*CONST["sinq"])] = np.tile(sin, (HEADS, 1)) * scale
    for name, t in (("cosk", cos), ("sink", sin)):
        halves = [np.tile(t[:, 512 * (i % 2):512 * (i % 2) + 512], (GROUPS, 1)) for i in range(4)]
        c[:, slice(*CONST[name])] = np.concatenate(halves)
    c[:, slice(*CONST["prio"])] = np.arange(E, 0, -1)
    key, query = np.meshgrid(np.arange(P), np.arange(P))
    mask = np.zeros((P, 512), np.float32)
    mask[:, 384:] = np.where(key > query, np.float32(MASKED), np.float32(0))
    c[:, slice(*CONST["mask"])] = mask
    return c


def kernel(**inputs):
    import ml_dtypes
    import numpy as np
    import concourse.bacc as _bacc
    from concourse import mybir as _mybir
    from concourse.bass_utils import run_bass_kernel_spmd as _run

    a = {k.replace("L0_attn_", "").replace("L0_ffn_", ""): np.asarray(v) for k, v in inputs.items()}
    swap = np.arange(D) ^ 1
    pack = np.zeros((P, PACK_N), np.float32)
    wide = {"Wq": a["Wq"], "Wqr": a["Wq"][:, swap], "Wk": a["Wk"], "Wkr": a["Wk"][:, swap[:32]],
            "Wvg": np.concatenate([a["Wv"], a["Wg"].T], axis=1), "bq": a["bq"][:, None], "bqr": a["bq"][swap][:, None],
            "bk": np.tile(a["bk"], 4)[:, None], "bkr": np.tile(a["bk"][swap[:32]], 4)[:, None],
            "bv": np.tile(a["bv"][None], (P, 1)), "Wo": a["Wo"], "bo": np.tile(a["bo"][None], (P, 1))}
    for name, w in wide.items():
        pack[:, slice(*PACK[name])] = w
    pack[0:E, slice(*PACK["b3"])] = a["b3"]
    wa = np.concatenate([a["W1"].transpose(0, 2, 1), a["W2"].transpose(0, 2, 1),
                         a["b1"].reshape(E, 2, P).transpose(0, 2, 1), a["b2"].reshape(E, 2, P).transpose(0, 2, 1)],
                        axis=2)
    wd = a["W3"].transpose(0, 2, 1).reshape(E, 2, P, D).transpose(0, 2, 1, 3).reshape(E, P, 2 * D)
    rows = np.zeros((2 * PARTS, HPG * T), ml_dtypes.bfloat16)
    rows[PARTS:] = -1
    arrays = {"x": a["x"], "pack": pack, "const": _tables(), "wa": wa, "wd": wd, "rows": rows}
    arrays = {f"in_{k}": np.ascontiguousarray(v) for k, v in arrays.items()}

    nc = _bacc.Bacc("TRN2", target_bir_lowering=False, num_devices=1)
    args = [nc.dram_tensor(n, v.shape, _mybir.dt.from_np(v.dtype), kind="ExternalInput").ap()
            for n, v in arrays.items()]
    args.append(nc.dram_tensor("out_x", (B, T, D), F32, kind="ExternalOutput").ap())
    attention_and_experts(nc, *args)
    return _run(nc, [arrays], core_ids=[0]).results[0]["out_x"]
```

```python
from contextlib import ExitStack

import concourse.bass as bass
from concourse import mybir

ALU = mybir.AluOpType
ACT = mybir.ActivationFunctionType
F32 = mybir.dt.float32
F32R = mybir.dt.float32r
BF16 = mybir.dt.bfloat16
AX_X = mybir.AxisListType.X

P = 128
B, T, D = 2, 1024, 128
HEADS, GROUPS, DH = 16, 4, 8
HPG = HEADS // GROUPS
E, DFF = 8, 256
TB = T // P
NTB = B * TB
NG = B * GROUPS
EPS = 1e-5
MASKED = -1e30
PARTS = 3
M_ROW = PARTS * PARTS * DH

PACK = {}
_at = 0
for _name, _n in (("Wq", 128), ("Wqr", 128), ("Wk", 32), ("Wkr", 32), ("Wvg", 40), ("bq", 1), ("bqr", 1), ("bk", 1),
                  ("bkr", 1), ("bv", 32), ("Wo", 128), ("bo", 128), ("b3", 128)):
    PACK[_name] = (_at, _at + _n)
    _at += _n
PACK_N = _at
CONST = {}
_at = 0
for _name, _n in (("ident", 128), ("cosk", 512), ("sink", 512), ("prio", 8), ("cosq", 1024), ("sinq", 1024),
                  ("mask", 512)):
    CONST[_name] = (_at, _at + _n)
    _at += _n
CONST_N = _at
CONST_FIRST = CONST["ident"][1]

UNITS = 36
STEPS = 10
STEP_PARTS = [
    [(0, 0, 512)],
    [(1, 128, 384), (3, 384, 128)],
    [(2, 256, 256)],
    [(0, 512, 512)],
    [(1, 512, 512)],
    [(2, 512, 512)],
    [(3, 512, 512)],
    [(4, 512, 512)],
    [(5, 640, 384), (7, 896, 128)],
    [(6, 768, 256)],
]
P_UNITS = []
STEP_LAST_UNIT = []
STEP_OF_UNIT = []
for _s, _parts in enumerate(STEP_PARTS):
    if sum(p[2] for p in _parts) == 512:
        for _h in range(HPG):
            _c = 0
            _u = []
            for _j, _t0, _n in _parts:
                _u.append((_h, _j, _t0, _n, _c))
                _c += _n
            P_UNITS.append(_u)
            STEP_OF_UNIT.append(_s)
    else:
        _j, _t0, _n = _parts[0]
        for _h in (0, 2):
            P_UNITS.append([(_h, _j, _t0, _n, 0), (_h + 1, _j, _t0, _n, _n)])
            STEP_OF_UNIT.append(_s)
    STEP_LAST_UNIT.append(len(P_UNITS) - 1)
assert len(P_UNITS) == UNITS
HAS_DIAGONAL = [any(t0 == j * P for j, t0, n in parts) for parts in STEP_PARTS]
MASKS = sum(HAS_DIAGONAL)
S_UNITS = []
for _h in range(HPG):
    for _i in (3, 4, 5, 6, 7):
        S_UNITS.append([(_h, _i, 0, 512, 0)])
    S_UNITS.append([(_h, 7, 512, 512, 0)])
    S_UNITS.append([(_h, 0, 0, 128, 0), (_h, 2, 0, 384, 128)])
    S_UNITS.append([(_h, 4, 512, 128, 0), (_h, 6, 512, 384, 128)])
    S_UNITS.append([(_h, 1, 0, 256, 0), (_h, 5, 512, 256, 256)])
assert len(S_UNITS) == UNITS
RING_PER_GROUP = UNITS + 3
CHUNKS = 8
CHUNK = B * T // CHUNKS

POSITIONS = 40
PV_AT = {7: 0, 9: 1, 12: 2, 16: 3, 19: 4, 24: 5, 28: 6, 31: 7, 34: 8, 36: 9}
EVAC_AT = {13: 0, 35: 1}
OT_AT = {16: 0, 38: 1}
M_AT = 33
MOE_ITEMS = []
for _c in range(CHUNKS):
    MOE_ITEMS += [(_c, "up0"), (_c, "up1")] + ([(_c - 1, "down")] if _c else [])
MOE_ITEMS.append((CHUNKS - 1, "down"))
MOE_INDEX = {_item: _i for _i, _item in enumerate(MOE_ITEMS)}


def _spread(first, last, n):
    at = {}
    span = last - first + 1
    for i in range(n):
        at.setdefault(first + i * span // n, []).append(i)
    return at


S_AT = _spread(3, 31, UNITS)
P_AT = _spread(0, 33, UNITS)
LAST_P_AT = _spread(0, 27, UNITS)
MOE_POSITION = [0, 0, 2, 4, 6, 8, 9, 11, 12, 14, 15, 17, 19, 20, 22, 24, 26, 27, 28, 30, 31, 33, 34, 39]
MOE_AT = {}
for _i, _item in enumerate(MOE_ITEMS):
    MOE_AT.setdefault(MOE_POSITION[_i], []).append(_item)
UP_LATER, DOWN_LATER = 2, 1
H_LATER = 1

FIRST_SPAN = UNITS + 8
FIRST_MOE_AT = {_p: [MOE_ITEMS[_i] for _i in _which]
                for _p, _which in _spread(0, FIRST_SPAN - 2, len(MOE_ITEMS)).items()}
FIRST_TURN_AT = UNITS + 1
FIRST_LATER = 1
Q1_ROUND_AT = (0, 1, 4)
Q1_LAST_AT = 2
COMB_AT = (12, 18, 20, 26)
BIAS_AT = (36, 38, 40, 42)


def up_count(c, f):
    return 2 * c + f + 1


TAIL_AT = {1: [("turn", 0, 0)], 4: [("turn", 0, 1)], 6: [("project", 0, 0)], 10: [("project", 0, 1)],
           20: [("turn", 1, 0)], 24: [("project", 1, 0)]}
TAIL_END = [("turn", 1, 1, 0), ("turn", 1, 1, 1), ("project", 1, 1, 0), ("project", 1, 1, 1)]
TAIL_INDEX = {}
_i = 0
for _p in range(POSITIONS):
    for _w in TAIL_AT.get(_p, []) + ([("outputs", 1, OT_AT[_p])] if _p in OT_AT else []):
        TAIL_INDEX[_w] = _i
        _i += 1
for _w in TAIL_END:
    TAIL_INDEX[_w] = _i
    _i += 1


def blocks_of(part):
    return (2 * part[0], 2 * part[0] + 2) if part else (0, 4)


def attention_and_experts(nc, x, pack, const, wa, wd, zrow, out):
    q_dram = nc.dram_tensor("q_parts", (NG, PARTS, DH, HPG * T), BF16).ap()
    k_dram = nc.dram_tensor("k_parts", (NG, PARTS, DH, T), BF16).ap()

    with ExitStack() as ctx:
        def sb(name, shape, dt=F32):
            return ctx.enter_context(nc.sbuf_tensor(name, shape, dt))

        def sem(name):
            return ctx.enter_context(nc.semaphore(name))

        pk = sb("pk", [P, PACK_N])
        cn = sb("cn", [P, CONST_N])
        xs = sb("xs", [P, NTB, D])
        junk = xs[:, :, :].rearrange("p (n i) c -> p n (i c)", n=4)
        acc = sb("acc", [P, NTB, D])
        stats = sb("stats", [P, NTB, 6])
        meanvar = sb("meanvar", [P, NTB, 2])
        rstd = sb("rstd", [P, NTB])
        deviation = sb("deviation", [P, NTB])
        xT = sb("xT", [P, B * T])
        xh = sb("xh", [P, B * T], F32R)
        xl = sb("xl", [P, B * T], F32R)
        q_part = sb("q_part", [P, PARTS, T], BF16)
        krope_a = sb("krope_a", [P, 512])
        krope_b = sb("krope_b", [P, 512])
        k_part = sb("k_part", [P, PARTS, 512], BF16)
        qs = sb("qs", [P, 2, HPG * T], BF16)
        ks = sb("ks", [P, 2, T], BF16)
        vt = sb("vt", [P, NG, TB, 32])
        vcur = sb("vcur", [P, 2, TB, 32])
        pt = sb("pt", [P, 4, HPG * 512])
        rope_a, rope_b = pt[:, 3, 0:T], pt[:, 3, T:2 * T]
        q_part_b = [q_part, pt[:, 2, 0:PARTS * T // 2].bitcast(BF16).rearrange("p (a t) -> p a t", a=PARTS)]
        mx = sb("mx", [P, HPG, TB])
        mx_a = sb("mx_a", [P, HPG, 4])
        mx_b = sb("mx_b", [P, HPG, 4])
        mrow = sb("mrow", [HPG * TB, PARTS, P], BF16)
        mres = sb("mres", [HPG * TB, 2, P])
        o_t = sb("o_t", [P, 2, 512])
        rl = sb("rl", [P, 2, 16])
        on = sb("on", [P, TB, NG // 2, 2 * HPG * DH])
        xn = sb("xn", [P, NTB, D])
        on_t = xn[:, :, :].rearrange("p (b i) c -> p b i c", b=B)
        gate = sb("gate", [P, NTB, E])
        gtmp = sb("gtmp", [P, 5, NTB, E])
        gcol = sb("gcol", [P, 6, NTB])
        comb = sb("comb", [P, E, NTB])
        comb_cur = sb("comb_cur", [P, 2, NTB])
        comb_t = sb("comb_t", [E, B * T])
        w_raw = sb("w_raw", [P, 2, 2 * DFF + 4])
        w_h = sb("w_h", [P, 2, 2 * DFF], F32R)
        w_l = sb("w_l", [P, 2, 2 * DFF], F32R)
        w_down = sb("w_down", [P, 2, 2 * D])
        half_b1 = sb("half_b1", [P, 2, 2])
        th = sb("th", [P, 2, 2, CHUNK])
        zz = sb("zz", [P, 2, 2, CHUNK])
        h_part = sb("h_part", [P, 2, CHUNK])
        hh = sb("hh", [P, 2, 2, CHUNK])
        bank = [ctx.enter_context(nc.psum_tensor(f"bank{i}", [P, 512], F32)) for i in range(8)]
        p_bank = bank[0:2]
        last_p_bank = bank[0:2] + bank[6:8]
        r_bank = bank[2:5]
        o_bank = bank[5]
        m_bank = [bank[6], bank[7], bank[5]]

        def pkc(name, rows=P):
            a, b = PACK[name]
            return pk[0:rows, a:b]

        def cnc(name):
            a, b = CONST[name]
            return cn[:, a:b]

        ident = cnc("ident")

        x_loaded = [sem(f"x_loaded{b}") for b in range(B)]
        pack_loaded = sem("pack_loaded")
        ident_loaded = sem("ident_loaded")
        tables_loaded = sem("tables_loaded")
        var_due = sem("var_due")
        deviation_done = sem("deviation_done")
        xn_done = sem("xn_done")
        xT_made = sem("xT_made")
        xT_done = sem("xT_done")
        xh_done = sem("xh_done")
        xl_done = sem("xl_done")
        q_made = sem("q_made")
        q_taken = sem("q_taken")
        k_made = sem("k_made")
        k_taken = sem("k_taken")
        vg_made = sem("vg_made")
        part_due = sem("part_due")
        part_done = sem("part_done")
        q_stored = [sem(f"q_stored{b}") for b in range(B)]
        q_first = sem("q_first")
        k_stored = [sem(f"k_stored{b}") for b in range(B)]
        gate_due = sem("gate_due")
        gate_exp = sem("gate_exp")
        comb_done = sem("comb_done")
        v_made = sem("v_made")
        comb_turned = sem("comb_turned")
        comb_t_done = sem("comb_t_done")
        bias_made = sem("bias_made")
        bias_added = sem("bias_added")
        acc_begun = sem("acc_begun")
        cleared = sem("cleared")
        own = sem("own")
        stack_loaded = sem("stack_loaded")
        v_loaded = sem("v_loaded")
        w_loaded = [sem(f"w_loaded{par}") for par in range(2)]
        w_split = sem("w_split")
        comb_copied = sem("comb_copied")
        m_loaded = sem("m_loaded")
        minus_loaded = sem("minus_loaded")
        p_full = sem("p_full")
        exp_done = sem("exp_done")
        mask_done = sem("mask_done")
        pv_step = sem("pv_step")
        o_copied = sem("o_copied")
        r_full = sem("r_full")
        r_free = sem("r_free")
        mx_done = sem("mx_done")
        mrow_done = sem("mrow_done")
        up_made = sem("up_made")
        tanh_made = sem("tanh_made")
        act_made = sem("act_made")
        factor_made = sem("factor_made")
        h_begun = sem("h_begun")
        h_made = sem("h_made")
        down_made = sem("down_made")
        acc_added = sem("acc_added")
        stored = sem("stored")
        P_CREDIT, R_CREDIT, PT_CREDIT, O_CREDIT, ACC_CREDIT = 2, 3, 4, 1, 2

        waited = sem("waited")
        STACK_DMAS = PARTS + 1 + 1
        PART_BASE = {"q0": 0, "k": 2 * PARTS, "q1": 3 * PARTS}

        block = ctx.enter_context(nc.Block())

        def wait_apart(eng, semaphore, value):
            eng.wait_ge(semaphore, value)
            eng.sem_inc(waited, 1)

        @block.sync
        def _(sp):
            def load_stack_q(m, par):
                for a in range(PARTS):
                    r = a * PARTS * DH
                    sp.dma_start(qs[r:r + PARTS * DH, par, :],
                                 q_dram[bass.ds(m, 1), a].to_broadcast([PARTS, DH, HPG * T])).then_inc(stack_loaded, 16)
                sp.dma_start(qs[M_ROW:M_ROW + PARTS, par, :], zrow[0:PARTS, :]).then_inc(stack_loaded, 16)

            def load_stack_k(m, par):
                sp.dma_start(ks[0:M_ROW, par, :],
                             k_dram[bass.ds(m, 1)].rearrange("o a d t -> o (a d) t")
                             .to_broadcast([PARTS, PARTS * DH, T])).then_inc(stack_loaded, 16)

            def load_v(m, par):
                sp.dma_start(vcur[:, par].rearrange("p j c -> p (j c)"),
                             vt[:, bass.ds(m, 1)].rearrange("p o j c -> p (o j c)")).then_inc(v_loaded, 16)

            def load_expert(m, par):
                sp.dma_start(w_raw[:, par, :], wa[bass.ds(m, 1)].rearrange("o p c -> (o p) c")).then_inc(w_loaded[par], 16)
                sp.dma_start(w_down[:, par, :], wd[bass.ds(m, 1)].rearrange("o p c -> (o p) c")).then_inc(w_loaded[par], 16)

            def load_maxima(m, par):
                sp.wait_ge(mrow_done, m + 1)
                for c in range(PARTS):
                    sp.dma_start(qs[M_ROW + c:M_ROW + c + 1, par, :], mrow[:, c, :]).then_inc(m_loaded, 16)

            def group(n, half, experts):
                sp.wait_ge(exp_done, n * UNITS + P_CREDIT)
                load_stack_q(n + 1, 1 - half)
                load_stack_k(n + 1, 1 - half)
                sp.wait_ge(pv_step, n * STEPS + PT_CREDIT)
                load_v(n + 1, 1 - half)
                if experts:
                    sp.wait_ge(acc_added, n * CHUNKS + CHUNKS + ACC_CREDIT)
                    load_expert(n + 2, half)
                load_maxima(n + 1, 1 - half)

            for b in range(B):
                sp.dma_start(xs[:, b * TB:(b + 1) * TB, :], x[b].rearrange("(i p) c -> p i c", p=P))\
                    .then_inc(x_loaded[b], 16)
                if b == 0:
                    sp.dma_start(pk[:, :], pack).then_inc(pack_loaded, 16)
            sp.dma_start(cn[:, CONST_FIRST:CONST_N], const[:, CONST_FIRST:CONST_N]).then_inc(tables_loaded, 16)
            for e in range(2):
                load_expert(e, e)
            sp.wait_ge(cleared, 2)
            for par in range(2):
                sp.dma_start(ks[M_ROW:M_ROW + PARTS, par, :], zrow[PARTS:2 * PARTS, 0:T]).then_inc(minus_loaded, 16)
            def store_q(b, g):
                for a in range(PARTS):
                    dst = q_dram[GROUPS * b + g, a].rearrange("d (h t) -> h d t", h=HPG)
                    sp.dma_start(dst, q_part_b[b][32 * g:32 * (g + 1), a, :]).then_inc(q_first if b + g == 0 else q_stored[b], 16)

            def store_k(b):
                for a in range(PARTS):
                    sp.wait_ge(part_done, PART_BASE["k"] + a + 1)
                    for half in range(2):
                        c = 2 * b + half
                        dst = k_dram[GROUPS * b:GROUPS * (b + 1), a, :, half * 512:(half + 1) * 512]
                        sp.dma_start(dst, k_part[32 * c:32 * (c + 1), a, :]).then_inc(k_stored[b], 16)

            sp.wait_ge(part_done, PART_BASE["q0"] + 2 * PARTS)
            store_q(0, 0)
            store_k(0)
            sp.wait_ge(q_first, 16 * PARTS)
            load_stack_q(0, 0)
            sp.wait_ge(k_stored[0], 16 * 2 * PARTS)
            load_stack_k(0, 0)
            for g in range(1, GROUPS):
                store_q(0, g)
            store_k(1)
            sp.wait_ge(v_made, 2)
            load_v(0, 0)
            sp.wait_ge(q_stored[0], 16 * (GROUPS - 1) * PARTS)
            sp.wait_ge(k_stored[1], 16 * 2 * PARTS)
            sp.wait_ge(part_done, PART_BASE["q1"] + 2 * PARTS)
            for g in range(GROUPS):
                store_q(1, g)
            sp.wait_ge(q_stored[1], 16 * GROUPS * PARTS)
            load_maxima(0, 0)
            with sp.Fori(0, NG // 2 - 1) as k:
                for half in range(2):
                    group(2 * k + half, half, True)
            group(NG - 2, 0, False)
            for what in ((0, 0), (0, 1), (1, 0), (1, 1, 0), (1, 1, 1)):
                b, i, *part = what
                sp.wait_ge(r_free, NG * RING_PER_GROUP + TAIL_INDEX[("project",) + what] + 1 + R_CREDIT)
                lo, hi = blocks_of(part)
                sp.dma_start(out[b, 512 * i + P * lo:512 * i + P * hi].rearrange("(i p) c -> p i c", p=P),
                             acc[:, TB * b + 4 * i + lo:TB * b + 4 * i + hi, :]).then_inc(stored, 16)
            sp.wait_ge(stored, 16 * 5)

        @block.gpsimd
        def _(pool):
            def split_expert(m, par, turn):
                wait_apart(pool, w_loaded[par], 32 * (turn + 1))
                pool.tensor_copy(w_h[:, par, :], w_raw[:, par, 0:2 * DFF]).then_inc(w_split, 1)
                pool.tensor_scalar(half_b1[:, par, :], w_raw[:, par, 2 * DFF:2 * DFF + 2], 0.5, None, ALU.mult)\
                    .then_inc(w_split, 1)
                pool.wait_ge(w_split, 3 * m + 1)
                pool.tensor_tensor(w_l[:, par, :], w_raw[:, par, 0:2 * DFF], w_h[:, par, :].bitcast(F32),
                                   ALU.subtract).then_inc(w_split, 1)

            def tokens_weights(m, par):
                pool.tensor_copy(comb_cur[:, par, :], comb[:, bass.ds(m, 1), :].rearrange("p o i -> p (o i)"))\
                    .then_inc(comb_copied, 1)

            def mask(n, half, s):
                wait_apart(pool, exp_done, n * UNITS + STEP_LAST_UNIT[s] + 1 + P_CREDIT)
                width = sum(w for _, _, w in STEP_PARTS[s])
                c = 0
                for _, _, w in STEP_PARTS[s]:
                    v = pt[:, (half * STEPS + s) % 4, 0:HPG * width].rearrange("p (h c) -> p h c", h=HPG)[:, :, c:c + P]
                    ins = pool.affine_select(out=v, in_=v, compare_op=ALU.is_ge, fill=0.0, base=0,
                                             pattern=[[0, HPG], [1, P]], channel_multiplier=-1)
                    c += w
                ins.then_inc(mask_done, 1)

            def expert_h(m, c, f):
                h = hh[:, c % 2, f, :]
                pool.wait_ge(factor_made, m * 2 * CHUNKS + up_count(c, f))
                pool.tensor_tensor(h_part[:, f, :], th[:, c % 2, f, :], h, ALU.mult).then_inc(h_begun, 1)
                pool.wait_ge(h_begun, m * 2 * CHUNKS + up_count(c, f))
                pool.tensor_tensor(h, h_part[:, f, :], h, ALU.add).then_inc(h_made, 1)

            def first_expert_h(c, f):
                h = hh[:, c % 2, f, :]
                pool.wait_ge(factor_made, up_count(c, f))
                pool.tensor_tensor(h_part[:, f, :], th[:, c % 2, f, :], zz[:, c % 2, f, :], ALU.mult)\
                    .then_inc(h_begun, 1)
                pool.wait_ge(h_begun, up_count(c, f))
                pool.tensor_tensor(h, h_part[:, f, :], h, ALU.mult).then_inc(h_made, 1)

            def group(n, half, front, k=None):
                for pos in range(POSITIONS):
                    for s in range(STEPS):
                        if STEP_LAST_UNIT[s] in (P_AT if front else LAST_P_AT).get(pos, []) and HAS_DIAGONAL[s]:
                            mask(n, half, s)
                    if front:
                        for c, kind in MOE_AT.get(pos - H_LATER, []):
                            if kind != "down":
                                expert_h(n + 1, c, int(kind[2]))
                    if k is not None and pos == 12:
                        split_expert(n + 2, half, k + 1)
                        tokens_weights(n + 2, half)
                if front:
                    for pos in range(POSITIONS - H_LATER, POSITIONS):
                        assert all(kind == "down" for c, kind in MOE_AT.get(pos, []))

            pool.memset(qs[:, :, :].bitcast(F32), 0.0).then_inc(cleared, 1)
            pool.memset(ks[:, :, :].bitcast(F32), 0.0).then_inc(cleared, 1)
            pool.memset(vt[:, :, :, :], 0.0).then_inc(cleared, 1)
            pool.wait_ge(cleared, 3)
            pool.memset(vt[:, :, :, DH:DH + 1], 1.0).then_inc(cleared, 1)
            for b in range(B):
                pool.wait_ge(x_loaded[b], 16)
            pool.wait_ge(pack_loaded, 16)
            pool.tensor_tensor(acc[:, :, :], xs[:, :, :], pkc("bo").unsqueeze(1).to_broadcast([P, NTB, D]), ALU.add)\
                .then_inc(acc_begun, 1)
            for i in range(4):
                pool.wait_ge(xh_done, i + 1)
                pool.tensor_tensor(xl[:, 512 * i:512 * (i + 1)], xT[:, 512 * i:512 * (i + 1)],
                                   xh[:, 512 * i:512 * (i + 1)].bitcast(F32), ALU.subtract).then_inc(xl_done, 1)
            for e in range(2):
                split_expert(e, e, 0)
            for c in range(CHUNKS):
                for f in range(2):
                    first_expert_h(c, f)
                if c == 0:
                    pool.wait_ge(comb_done, 1)
                    for e in range(2):
                        tokens_weights(e, e)
            with pool.Fori(0, NG // 2 - 1) as k:
                for half in range(2):
                    group(2 * k + half, half, True, k)
            group(NG - 2, 0, True)
            group(NG - 1, 1, False)

        @block.scalar
        def _(act):
            def exp_unit(n, half, u, banks):
                s = STEP_OF_UNIT[u]
                first = STEP_LAST_UNIT[s - 1] + 1 if s else 0
                if u == first:
                    act.wait_ge(pv_step, n * STEPS + s + 1)
                act.wait_ge(p_full, n * UNITS + u + 1)
                at = (u - first) * 512
                nc.scalar.activation(pt[:, (half * STEPS + s) % 4, at:at + 512], banks[u % len(banks)][:, :], ACT.Exp)\
                    .then_inc(exp_done, 1)

            def expert_act(m, par, c, f):
                act.wait_ge(up_made, m * 2 * CHUNKS + 2 * c + f + 1)
                src = m_bank[MOE_INDEX[c, f"up{f}"] % 2][:, 0:CHUNK]
                nc.scalar.activation(th[:, c % 2, f, :], src, ACT.Tanh, bias=half_b1[:, par, f:f + 1], scale=0.5)
                nc.scalar.activation(zz[:, c % 2, f, :], src, ACT.Identity, bias=half_b1[:, par, f:f + 1], scale=0.5)\
                    .then_inc(act_made, 1)

            def first_expert_act(c, f):
                i = up_count(c, f)
                act.wait_ge(up_made, i)
                src = m_bank[MOE_INDEX[c, f"up{f}"] % 3]
                nc.scalar.activation(th[:, c % 2, f, :], src[:, 0:CHUNK], ACT.Tanh, bias=half_b1[:, 0, f:f + 1],
                                     scale=0.5).then_inc(tanh_made, 1)
                nc.scalar.activation(zz[:, c % 2, f, :], src[:, 0:CHUNK], ACT.Identity, bias=half_b1[:, 0, f:f + 1],
                                     scale=0.5).then_inc(act_made, 1)
                act.wait_ge(tanh_made, i)
                nc.scalar.activation(th[:, c % 2, f, :], th[:, c % 2, f, :], ACT.Identity,
                                     bias=vt[:, 0, 0, DH:DH + 1], scale=1.0)
                nc.scalar.activation(hh[:, c % 2, f, :], src[:, CHUNK:2 * CHUNK], ACT.Identity,
                                     bias=w_raw[:, 0, 2 * DFF + 2 + f:2 * DFF + 3 + f], scale=1.0)\
                    .then_inc(factor_made, 1)

            def copy_outputs(n, x):
                act.wait_ge(pv_step, n * STEPS + (3, STEPS)[x] + PT_CREDIT)
                nc.scalar.copy(o_t[:, x, :], o_bank[:, :]).then_inc(o_copied, 1)

            def group(n, half, front):
                for pos in range(POSITIONS):
                    for u in (P_AT if front else LAST_P_AT).get(pos, []):
                        exp_unit(n, half, u, p_bank if front else last_p_bank)
                    if front:
                        for c, kind in MOE_AT.get(pos, []):
                            if kind != "down":
                                expert_act(n + 1, 1 - half, c, int(kind[2]))
                    if pos in EVAC_AT:
                        copy_outputs(n, EVAC_AT[pos])

            act.dma_start(cn[:, 0:CONST_FIRST], const[:, 0:CONST_FIRST]).then_inc(ident_loaded, 16)
            act.sem_inc(exp_done, P_CREDIT)
            act.sem_inc(o_copied, O_CREDIT)
            for b in range(B):
                act.wait_ge(var_due, b + 1)
                nc.scalar.activation(deviation[:, TB * b:TB * (b + 1)], rstd[:, TB * b:TB * (b + 1)], ACT.Sqrt)\
                    .then_inc(deviation_done, 1)
                for i in (2 * b, 2 * b + 1):
                    act.wait_ge(xT_made, i + 1)
                    nc.scalar.copy(xT[:, 512 * i:512 * (i + 1)], bank[i][:, :]).then_inc(xT_done, 1)
            def round_q(b, a):
                for c in range(2):
                    act.wait_ge(part_due, PART_BASE[f"q{b}"] + 2 * a + c + 1)
                    half = slice(512 * c, 512 * (c + 1))
                    nc.scalar.copy(q_part_b[b][:, a, half], rope_a[:, half]).then_inc(part_done, 1)

            def high_part(i):
                nc.scalar.copy(xh[:, 512 * i:512 * (i + 1)], xT[:, 512 * i:512 * (i + 1)]).then_inc(xh_done, 1)

            act.wait_ge(xT_done, 4)
            for a in range(PARTS):
                round_q(0, a)
                high_part(a)
            high_part(3)
            for a in range(PARTS):
                act.wait_ge(part_due, PART_BASE["k"] + a + 1)
                nc.scalar.copy(k_part[:, a, :], krope_a[:, :]).then_inc(part_done, 1)
            act.wait_ge(gate_due, 1)
            nc.scalar.activation(gcol[:, 3, :], gcol[:, 2, :], ACT.Exp).then_inc(gate_exp, 1)
            for u in range(FIRST_SPAN):
                if u in Q1_ROUND_AT:
                    round_q(1, Q1_ROUND_AT.index(u))
                for c, kind in FIRST_MOE_AT.get(u, []):
                    if kind != "down":
                        first_expert_act(c, int(kind[2]))
                if u in COMB_AT:
                    i = COMB_AT.index(u)
                    act.wait_ge(comb_turned, i + 1)
                    nc.scalar.copy(comb_t[:, 512 * i:512 * (i + 1)], bank[i % 2][0:E, :]).then_inc(comb_t_done, 1)
            act.wait_ge(q_stored[1], 16 * GROUPS * PARTS)
            with act.Fori(0, NG // 2 - 1) as k:
                for half in range(2):
                    group(2 * k + half, half, True)
            group(NG - 2, 0, True)
            group(NG - 1, 1, False)

        @block.vector
        def _(dve):
            steps = [0]

            def link(ins):
                ins.then_inc(own, 1)
                steps[0] += 1
                dve.wait_ge(own, steps[0])

            ring = {}

            def score_unit(m, u, r):
                wait_apart(dve, r_full, m_ring(m) + r + 1)
                b = r_bank[r % len(r_bank)]
                for h, i, s0, w, c in S_UNITS[u]:
                    src = b[:, c:c + w]
                    if i < 4:
                        dst = mx[:, h, i:i + 1]
                    else:
                        dst = (mx_b if s0 else mx_a)[:, h, i - 4:i - 3]
                    if s0 + w == (i + 1) * P:
                        ins = dve.tensor_tensor_reduce(junk[:, r % len(r_bank), c:c + w], src, cnc("mask")[:, 512 - w:512],
                                                       1.0, MASKED, ALU.add, ALU.max, dst)
                    else:
                        ins = dve.tensor_reduce(dst, src, AX_X, ALU.max)
                ins.then_inc(r_free, 1)

            def m_ring(m):
                return m * RING_PER_GROUP

            def group_maxima(m):
                dve.wait_ge(r_free, m_ring(m) + ring["last_score"] + 1 + R_CREDIT)
                dve.tensor_tensor(mx[:, :, 4:8], mx_a[:, :, :], mx_b[:, :, :], ALU.max).then_inc(mx_done, 1)

            def maxima_rows(m, r, taken=1):
                dve.wait_ge(r_full, m_ring(m) + r + 1)
                src = r_bank[r % len(r_bank)][0:HPG * TB, 0:P]
                base = 3 * m
                dve.tensor_copy(mrow[:, 0, :], src).then_inc(mstep, 1)
                dve.wait_ge(mstep, base + 1)
                dve.tensor_tensor(mres[:, 0, :], src, mrow[:, 0, :], ALU.subtract).then_inc(r_free, taken)
                dve.wait_ge(r_free, m_ring(m) + r + taken + R_CREDIT)
                dve.tensor_copy(mrow[:, 1, :], mres[:, 0, :]).then_inc(mstep, 1)
                dve.wait_ge(mstep, base + 2)
                dve.tensor_tensor(mres[:, 1, :], mres[:, 0, :], mrow[:, 1, :], ALU.subtract).then_inc(mstep, 1)
                dve.wait_ge(mstep, base + 3)
                dve.tensor_copy(mrow[:, 2, :], mres[:, 1, :]).then_inc(mrow_done, 1)

            mstep = sem("mstep")
            rlstep = sem("rlstep")

            def outputs(m, r, n, k, half, x):
                dve.wait_ge(r_full, m_ring(m) + r + 1)
                src = r_bank[r % len(r_bank)][:, :].rearrange("p (i h c) -> p i h c", i=4, h=HPG)
                flat = r_bank[r % len(r_bank)][:, :].rearrange("p (q c) -> p q c", c=32)
                dve.reciprocal(rl[:, x, :], flat[:, :, DH]).then_inc(rlstep, 1)
                dve.wait_ge(rlstep, 2 * n + x + 1)
                dst = on[:, 4 * x:4 * x + 4, bass.ds(k, 1), 32 * half:32 * half + 32]
                dst = dst.rearrange("p i o (h d) -> p (i o) h d", h=HPG)
                inv = rl[:, x, :].rearrange("p (i h) -> p i h", i=4).unsqueeze(3).to_broadcast([P, 4, HPG, DH])
                dve.tensor_tensor(dst, src[:, :, :, 0:DH], inv, ALU.mult).then_inc(r_free, 1)

            def expert_factor(m, par, c, f):
                dve.wait_ge(act_made, m * 2 * CHUNKS + up_count(c, f))
                dve.scalar_tensor_tensor(out=hh[:, c % 2, f, :],
                                         in0=m_bank[MOE_INDEX[c, f"up{f}"] % 2][:, CHUNK:2 * CHUNK],
                                         scalar=w_raw[:, par, 2 * DFF + 2 + f:2 * DFF + 3 + f], in1=zz[:, c % 2, f, :],
                                         op0=ALU.add, op1=ALU.mult).then_inc(factor_made, 1)

            def expert_add(m, par, c, banks):
                if c == 0:
                    dve.wait_ge(comb_copied, m + 1)
                dve.wait_ge(down_made, m * CHUNKS + c + 1)
                for i in range(2):
                    t = 2 * c + i
                    ins = dve.scalar_tensor_tensor(out=acc[:, t, :], in0=m_bank[MOE_INDEX[c, "down"] % banks][:, D * i:D * (i + 1)],
                                                   scalar=comb_cur[:, par, t:t + 1], in1=acc[:, t, :],
                                                   op0=ALU.mult, op1=ALU.add)
                ins.then_inc(acc_added, 1)

            def moe(m, par, items, banks=2):
                for c, kind in items:
                    if kind == "down":
                        expert_add(m, par, c, banks)
                    else:
                        expert_factor(m, par, c, int(kind[2]))

            def due(pos):
                return ([w for w in MOE_AT.get(pos - UP_LATER, []) if w[1] != "down"]
                        + [w for w in MOE_AT.get(pos - DOWN_LATER, []) if w[1] == "down"])

            def group(n, k, half, front):
                m = n + 1
                r = 0
                for pos in range(POSITIONS):
                    if front:
                        moe(m, 1 - half, due(pos))
                    if front:
                        for u in S_AT.get(pos, []):
                            score_unit(m, u, r)
                            ring["last_score"] = r
                            r += 1
                        if pos == M_AT - 1:
                            group_maxima(m)
                        if pos == M_AT:
                            maxima_rows(m, r)
                            r += 1
                    if pos in OT_AT:
                        outputs(m, r, n, k, half, OT_AT[pos])
                        r += 1
                if front:
                    for pos in (POSITIONS, POSITIONS + 1):
                        moe(m, 1 - half, due(pos))

            dve.sem_inc(r_free, R_CREDIT)
            dve.sem_inc(acc_added, ACC_CREDIT)
            for b in range(B):
                lo, hi = b * TB, (b + 1) * TB
                dve.wait_ge(x_loaded[b], 16)
                for i in range(lo, hi):
                    ins = dve.bn_stats(stats[:, i, :], xs[:, i, :])
                link(ins)
                for i in range(lo, hi):
                    ins = dve.bn_aggr(meanvar[:, i, :], stats[:, i, :])
                link(ins)
                dve.tensor_scalar(rstd[:, lo:hi], meanvar[:, lo:hi, 1], EPS, None, ALU.add).then_inc(var_due, 1)
                dve.wait_ge(deviation_done, b + 1)
                link(dve.reciprocal(rstd[:, lo:hi], deviation[:, lo:hi]))
                for i in range(lo, hi):
                    ins = dve.tensor_scalar(xn[:, i, :], xs[:, i, :], meanvar[:, i, 0:1], rstd[:, i:i + 1],
                                            ALU.subtract, ALU.mult)
                ins.then_inc(xn_done, 1)
            dve.wait_ge(pack_loaded, 16)

            def rope(dst_a, dst_b, made, at, bank_q, bank_r, bias, bias_r, cos, sin):
                dve.wait_ge(made, at)
                dve.scalar_tensor_tensor(out=dst_a, in0=bank_q[:, :], scalar=pkc(bias), in1=cos, op0=ALU.add,
                                         op1=ALU.mult)
                return dve.scalar_tensor_tensor(out=dst_b, in0=bank_r[:, :], scalar=pkc(bias_r), in1=sin,
                                                op0=ALU.add, op1=ALU.mult)

            def rope_q(b, c, bank_q, bank_r):
                half = slice(512 * c, 512 * (c + 1))
                rope(rope_a[:, half], rope_b[:, half], q_made, 2 * b + c + 1, bank_q, bank_r, "bq", "bqr",
                     cnc("cosq")[:, half], cnc("sinq")[:, half]).then_inc(q_taken, 1)

            def part_q(b, a):
                for c in range(2):
                    half = slice(512 * c, 512 * (c + 1))
                    if a == 0:
                        dve.wait_ge(q_taken, 2 * b + c + 1)
                        other = rope_b[:, half]
                    else:
                        dve.wait_ge(part_done, PART_BASE[f"q{b}"] + 2 * (a - 1) + c + 1)
                        other = q_part_b[b][:, a - 1, half]
                    dve.tensor_tensor(rope_a[:, half], rope_a[:, half], other, ALU.subtract if a else ALU.add)\
                        .then_inc(part_due, 1)

            dve.wait_ge(tables_loaded, 16)
            for c in range(2):
                rope_q(0, c, bank[4 + c], bank[6 + c])
            for a in range(PARTS):
                part_q(0, a)
            rope(krope_a[:, :], krope_b[:, :], k_made, 1, bank[0], bank[1], "bk", "bkr", cnc("cosk"), cnc("sink"))\
                .then_inc(k_taken, 1)
            for b in range(B):
                dve.wait_ge(vg_made, b + 1)
                if b == 0:
                    dve.wait_ge(cleared, 4)
                src = bank[2 + b][:, 0:TB * 40].rearrange("p (j c) -> p j c", c=40)
                for g in range(GROUPS):
                    ins = dve.tensor_tensor(vt[:, GROUPS * b + g, :, 0:DH], src[:, :, DH * g:DH * (g + 1)],
                                            pkc("bv")[:, DH * g:DH * (g + 1)].unsqueeze(1).to_broadcast([P, TB, DH]),
                                            ALU.add)
                dve.tensor_copy(gate[:, TB * b:TB * (b + 1), :], src[:, :, 32:40]).then_inc(v_made, 1)

            def col(i):
                return gcol[:, i, :].unsqueeze(2).to_broadcast([P, NTB, E])

            def part_k(a):
                if a == 0:
                    dve.wait_ge(k_taken, 1)
                    other = krope_b[:, :]
                else:
                    dve.wait_ge(part_done, PART_BASE["k"] + a)
                    other = k_part[:, a - 1, :]
                dve.tensor_tensor(krope_a[:, :], krope_a[:, :], other, ALU.subtract if a else ALU.add)\
                    .then_inc(part_due, 1)

            def own_step(ins):
                ins.then_inc(own, 1)
                steps[0] += 1
                return steps[0]

            prio = cnc("prio").unsqueeze(1).to_broadcast([P, NTB, E])
            eq, first_one, second_one, rest = gtmp[:, 0], gtmp[:, 1], gtmp[:, 2], gtmp[:, 3]
            part_k(0)
            dve.wait_ge(v_made, 2)
            link(dve.tensor_reduce(gcol[:, 0, :], gate[:, :, :], AX_X, ALU.max))
            equal = own_step(dve.tensor_tensor(eq, gate[:, :, :], col(0), ALU.is_equal))
            part_k(1)
            dve.wait_ge(own, equal)
            link(dve.tensor_tensor(eq, eq, prio, ALU.mult))
            highest = own_step(dve.tensor_reduce(gcol[:, 4, :], eq, AX_X, ALU.max))
            part_k(2)
            dve.wait_ge(own, highest)
            one = own_step(dve.tensor_tensor(first_one, eq, col(4), ALU.is_equal))
            dve.wait_ge(part_done, PART_BASE["q0"] + 2 * PARTS)
            rope_q(1, 0, bank[0], bank[1])
            dve.wait_ge(own, one)
            removed = own_step(dve.scalar_tensor_tensor(out=rest, in0=first_one, scalar=-3e38, in1=gate[:, :, :],
                                                        op0=ALU.mult, op1=ALU.add))
            rope_q(1, 1, bank[4], bank[5])
            dve.wait_ge(own, removed)
            link(dve.tensor_reduce(gcol[:, 1, :], rest, AX_X, ALU.max))
            dve.tensor_tensor(gcol[:, 2, :], gcol[:, 1, :], gcol[:, 0, :], ALU.subtract).then_inc(gate_due, 1)
            link(dve.tensor_tensor(eq, rest, col(1), ALU.is_equal))
            link(dve.tensor_tensor(eq, eq, prio, ALU.mult))
            link(dve.tensor_reduce(gcol[:, 4, :], eq, AX_X, ALU.max))
            one = own_step(dve.tensor_tensor(second_one, eq, col(4), ALU.is_equal))
            part_q(1, 0)
            part_q(1, 1)

            def shares(u, last):
                dve.wait_ge(own, last)
                if u == 1:
                    dve.wait_ge(gate_exp, 1)
                    return own_step(dve.tensor_scalar(gcol[:, 5, :], gcol[:, 3, :], 1.0, None, ALU.add))
                if u == 2:
                    return own_step(dve.reciprocal(gcol[:, 0, :], gcol[:, 5, :]))
                if u == 3:
                    return own_step(dve.tensor_tensor(gcol[:, 1, :], gcol[:, 3, :], gcol[:, 0, :], ALU.mult))
                if u == 4:
                    dve.tensor_tensor(gtmp[:, 0], first_one, col(0), ALU.mult)
                    return own_step(dve.tensor_tensor(gtmp[:, 4], second_one, col(1), ALU.mult))
                dve.tensor_tensor(comb[:, :, :].rearrange("p e i -> p i e"), gtmp[:, 0], gtmp[:, 4], ALU.add)\
                    .then_inc(comb_done, 1)

            dve.wait_ge(acc_begun, 1)

            def first_due(u):
                return [w for w in FIRST_MOE_AT.get(u - FIRST_LATER, []) if w[1] == "down"]

            r = 0
            for u in range(UNITS):
                if u == Q1_LAST_AT:
                    part_q(1, 2)
                if 1 <= u <= 5:
                    one = shares(u, one)
                moe(0, 0, first_due(u), 3)
                score_unit(0, u, r)
                ring["last_score"] = r
                r += 1
            for u in range(UNITS, FIRST_SPAN + FIRST_LATER):
                if u == UNITS:
                    group_maxima(0)
                if u - 1 in BIAS_AT:
                    i = BIAS_AT.index(u - 1)
                    dve.wait_ge(acc_added, sum(w[1] == "down" for v in range(u) for w in first_due(v)) + ACC_CREDIT)
                    dve.wait_ge(bias_made, i + 1)
                    dst = acc[:, 4 * i:4 * i + 4, :].rearrange("p i c -> p (i c)")
                    dve.tensor_tensor(dst, dst, bank[i % 2][:, :], ALU.add).then_inc(bias_added, 1)
                    dve.wait_ge(bias_added, i + 1)
                if u == FIRST_TURN_AT:
                    maxima_rows(0, r, RING_PER_GROUP - UNITS)
                moe(0, 0, first_due(u), 3)

            with dve.Fori(0, NG // 2 - 1) as k:
                for half in range(2):
                    group(2 * k + half, k, half, True)
            group(NG - 2, NG // 2 - 1, 0, True)

            def tail(r, what):
                kind, b, i, *part = what
                lo, hi = blocks_of(part)
                dve.wait_ge(r_full, m_ring(NG) + r + 1)
                src = r_bank[r % len(r_bank)][:, P * lo:P * hi]
                if kind == "turn":
                    ins = dve.tensor_copy(on_t[:, b, 4 * i + lo:4 * i + hi, :].rearrange("p i c -> p (i c)"), src)
                else:
                    dst = acc[:, TB * b + 4 * i + lo:TB * b + 4 * i + hi, :].rearrange("p i c -> p (i c)")
                    ins = dve.tensor_tensor(dst, dst, src, ALU.add)
                ins.then_inc(r_free, 1)

            m = NG
            r = 0
            for pos in range(POSITIONS):
                for what in TAIL_AT.get(pos, []):
                    tail(r, what)
                    r += 1
                if pos in OT_AT:
                    outputs(m, r, NG - 1, NG // 2 - 1, 1, OT_AT[pos])
                    r += 1
            for what in TAIL_END:
                tail(r, what)
                r += 1

        @block.tensor
        def _(pe):
            def ring_fill(m, r):
                pe.wait_ge(r_free, m * RING_PER_GROUP + r + 1)
                return r_bank[r % len(r_bank)]

            def score_unit(m, par, u, r):
                if u == 0:
                    pe.wait_ge(stack_loaded, 16 * STACK_DMAS * (m + 1))
                dst = ring_fill(m, r)
                for h, i, s0, w, c in S_UNITS[u]:
                    q0 = h * T + i * P
                    mm = pe.matmul(dst[:, c:c + w], qs[:, par, q0:q0 + P], ks[:, par, s0:s0 + w], start=True,
                                   stop=True)
                mm.then_inc(r_full, 1)

            def turn_maxima(m, r, made=1):
                dst = ring_fill(m, r)
                pe.wait_ge(mx_done, m + 1)
                pe.transpose(dst[0:HPG * TB, 0:P], mx[:, :, :].rearrange("p h i -> p (h i)"), ident)\
                    .then_inc(r_full, made)

            def prob_unit(n, par, u, banks=p_bank):
                if u == 0:
                    pe.wait_ge(m_loaded, 16 * PARTS * (n + 1))
                if u == P_CREDIT and len(banks) > P_CREDIT:
                    pe.wait_ge(acc_added, NG * CHUNKS + ACC_CREDIT)
                ago = P_CREDIT if u < P_CREDIT else len(banks)
                pe.wait_ge(exp_done, n * UNITS + u - ago + 1 + P_CREDIT)
                for h, j, t0, w, c in P_UNITS[u]:
                    mm = pe.matmul(banks[u % len(banks)][:, c:c + w], ks[:, par, j * P:(j + 1) * P],
                                   qs[:, par, h * T + t0:h * T + t0 + w], start=True, stop=True)
                mm.then_inc(p_full, 1)

            def pv(n, par, s):
                x = 0 if s < 3 else 1
                if s == 0:
                    pe.wait_ge(v_loaded, 16 * (n + 1))
                if s in (0, 3):
                    pe.wait_ge(o_copied, 2 * n + x + 1)
                pe.wait_ge(exp_done, n * UNITS + STEP_LAST_UNIT[s] + 1 + P_CREDIT)
                if HAS_DIAGONAL[s]:
                    pe.wait_ge(mask_done, n * MASKS + sum(HAS_DIAGONAL[:s + 1]))
                parts = STEP_PARTS[s]
                width = sum(w for _, _, w in parts)
                c = 0
                for j, t0, w in parts:
                    for h in range(HPG):
                        at = h * width + c
                        mm = pe.matmul(o_bank[32 * h:32 * (h + 1), t0 - 512 * x:t0 - 512 * x + w],
                                       vcur[:, par, j, :], pt[:, (par * STEPS + s) % 4, at:at + w],
                                       start=(s in (0, 3)), stop=(s in (2, STEPS - 1)), skip_group_check=True)
                    c += w
                mm.then_inc(pv_step, 1)

            def turn_outputs(m, r, n, x):
                dst = ring_fill(m, r)
                pe.wait_ge(o_copied, 2 * n + x + 1 + O_CREDIT)
                for i in range(4):
                    mm = pe.transpose(dst[:, P * i:P * (i + 1)], o_t[:, x, P * i:P * (i + 1)], ident)
                mm.then_inc(r_full, 1)

            def free_bank(m, c, kind, banks):
                i = MOE_INDEX[c, kind]
                if i >= banks:
                    before, what = MOE_ITEMS[i - banks]
                    if what == "down":
                        pe.wait_ge(acc_added, m * CHUNKS + before + 1 + ACC_CREDIT)
                    else:
                        pe.wait_ge(factor_made, m * 2 * CHUNKS + up_count(before, int(what[2])))
                elif banks == 2:
                    pe.wait_ge(acc_added, m * CHUNKS + i - 1 + ACC_CREDIT)
                return m_bank[i % banks]

            def moe(m, par, items, banks=2):
                for c, kind in items:
                    if kind != "down":
                        f = int(kind[2])
                        if c == 0 and f == 0:
                            pe.wait_ge(w_split, 3 * (m + 1))
                        dst = free_bank(m, c, kind, banks)
                        tok = slice(CHUNK * c, CHUNK * (c + 1))
                        for i in range(2):
                            w = slice(DFF * i + P * f, DFF * i + P * (f + 1))
                            for a, (wt, xt) in enumerate(((w_h, xh), (w_h, xl), (w_l, xh))):
                                mm = pe.matmul(dst[:, CHUNK * i:CHUNK * (i + 1)], wt[:, par, w], xt[:, tok],
                                               start=(a == 0), stop=(a == 2))
                        mm.then_inc(up_made, 1)
                    else:
                        pe.wait_ge(h_made, m * 2 * CHUNKS + up_count(c, 1))
                        dst = free_bank(m, c, kind, banks)
                        for i in range(2):
                            for f in range(2):
                                mm = pe.matmul(dst[:, D * i:D * (i + 1)], hh[:, c % 2, f, P * i:P * (i + 1)],
                                               w_down[:, par, D * f:D * (f + 1)], start=(f == 0), stop=(f == 1))
                        mm.then_inc(down_made, 1)

            def group(n, half, front):
                m = n + 1
                r = 0
                for pos in range(POSITIONS):
                    for u in (P_AT if front else LAST_P_AT).get(pos, []):
                        prob_unit(n, half, u, p_bank if front else last_p_bank)
                    if front:
                        for u in S_AT.get(pos, []):
                            score_unit(m, 1 - half, u, r)
                            r += 1
                        if pos == M_AT:
                            turn_maxima(m, r)
                            r += 1
                        moe(m, 1 - half, MOE_AT.get(pos, []))
                    else:
                        for what in TAIL_AT.get(pos, []):
                            tail(r, what)
                            r += 1
                    if pos in PV_AT:
                        pv(n, half, PV_AT[pos])
                    if pos in OT_AT:
                        turn_outputs(m, r, n, OT_AT[pos])
                        r += 1
                if not front:
                    for what in TAIL_END:
                        tail(r, what)
                        r += 1

            def tail(r, what):
                kind, b, i, *part = what
                dst = ring_fill(NG, r)

                def taken(*w):
                    pe.wait_ge(r_free, NG * RING_PER_GROUP + TAIL_INDEX[w] + 1 + R_CREDIT)

                if kind == "turn" and b == 1:
                    taken("outputs", 1, i)
                if kind == "project":
                    taken("turn", b, i, *part)
                for j in range(*blocks_of(part)):
                    to = dst[:, P * j:P * (j + 1)]
                    if kind == "turn":
                        mm = pe.transpose(to, on[:, 4 * i + j, 2 * b:2 * b + 2, :].rearrange("p k c -> p (k c)"), ident)
                    else:
                        mm = pe.matmul(to, on_t[:, b, 4 * i + j, :], pkc("Wo"), start=True, stop=True)
                mm.then_inc(r_full, 1)

            pe.sem_inc(pv_step, PT_CREDIT)
            pe.wait_ge(ident_loaded, 16)

            def turn_tokens(i):
                pe.wait_ge(xn_done, i // 2 + 1)
                for j in range(4):
                    mm = pe.transpose(bank[i][:, P * j:P * (j + 1)], xn[:, 4 * i + j, :], ident)
                mm.then_inc(xT_made, 1)

            def make_q(b, c, bank_q, bank_r):
                tok = xT[:, T * b + 512 * c:T * b + 512 * (c + 1)]
                pe.matmul(bank_q[:, :], pkc("Wq"), tok, start=True, stop=True)
                pe.matmul(bank_r[:, :], pkc("Wqr"), tok, start=True, stop=True).then_inc(q_made, 1)

            for i in range(2):
                turn_tokens(i)
            pe.wait_ge(pack_loaded, 16)
            for c in range(2):
                pe.wait_ge(xT_done, c + 1)
                make_q(0, c, bank[4 + c], bank[6 + c])
            for i in range(2, 4):
                turn_tokens(i)
            pe.wait_ge(xT_done, 4)
            for i, w in ((0, "Wk"), (1, "Wkr")):
                for c in range(4):
                    mm = pe.matmul(bank[i][32 * c:32 * (c + 1), :], pkc(w), xT[:, 512 * c:512 * (c + 1)], start=True,
                                   stop=True)
            mm.then_inc(k_made, 1)
            for b in range(B):
                for j in range(TB):
                    t = TB * b + j
                    mm = pe.matmul(bank[2 + b][:, 40 * j:40 * (j + 1)], xT[:, P * t:P * (t + 1)], pkc("Wvg"),
                                   start=True, stop=True)
                mm.then_inc(vg_made, 1)

            pe.wait_ge(k_taken, 1)
            make_q(1, 0, bank[0], bank[1])
            pe.wait_ge(q_taken, 2)
            make_q(1, 1, bank[4], bank[5])

            pe.wait_ge(v_made, 2)
            pe.wait_ge(xl_done, 4)
            for u in range(FIRST_SPAN):
                if u == len(r_bank) - 1:
                    pe.wait_ge(q_taken, 4)
                moe(0, 0, FIRST_MOE_AT.get(u, []), 3)
                if u == 0:
                    pe.wait_ge(minus_loaded, 32)
                if u < UNITS:
                    score_unit(0, 0, u, u)
                if u == FIRST_TURN_AT:
                    turn_maxima(0, UNITS, RING_PER_GROUP - UNITS)
                if u in COMB_AT:
                    i = COMB_AT.index(u)
                    if i == 0:
                        pe.wait_ge(comb_copied, 2)
                    if i >= 2:
                        pe.wait_ge(comb_t_done, i - 1)
                    for j in range(4):
                        mm = pe.transpose(bank[i % 2][0:E, P * j:P * (j + 1)], comb[:, :, 4 * i + j], ident)
                    mm.then_inc(comb_turned, 1)
                if u in BIAS_AT:
                    i = BIAS_AT.index(u)
                    if i == 0:
                        pe.wait_ge(comb_t_done, 4)
                    if i >= 2:
                        pe.wait_ge(bias_added, i - 1)
                    for j in range(4):
                        mm = pe.matmul(bank[i % 2][:, P * j:P * (j + 1)],
                                       comb_t[:, P * (4 * i + j):P * (4 * i + j + 1)], pkc("b3", E), start=True,
                                       stop=True)
                    mm.then_inc(bias_made, 1)
            pe.wait_ge(bias_added, 4)
            pe.wait_ge(acc_added, CHUNKS + ACC_CREDIT)

            with pe.Fori(0, NG // 2 - 1) as k:
                for half in range(2):
                    group(2 * k + half, half, True)
            group(NG - 2, 0, True)
            group(NG - 1, 1, False)


def _tables():
    import numpy as np

    c = np.zeros((P, CONST_N), np.float32)
    c[:, slice(*CONST["ident"])] = np.eye(P, dtype=np.float32)
    freq = np.exp(-(np.arange(0, DH, 2, dtype=np.float32) / np.float32(DH)) * np.log(np.float32(10000.0)))
    angle = np.arange(T, dtype=np.float32)[:, None] * freq.astype(np.float32)
    cos = np.repeat(np.cos(angle), 2, axis=1).T
    sin = np.repeat(np.sin(angle), 2, axis=1).T * np.tile(np.array([-1, 1], np.float32), DH // 2)[:, None]
    scale = np.float32(1) / np.sqrt(np.float32(DH))
    c[:, slice(*CONST["cosq"])] = np.tile(cos, (HEADS, 1)) * scale
    c[:, slice(*CONST["sinq"])] = np.tile(sin, (HEADS, 1)) * scale
    for name, t in (("cosk", cos), ("sink", sin)):
        halves = [np.tile(t[:, 512 * (i % 2):512 * (i % 2) + 512], (GROUPS, 1)) for i in range(4)]
        c[:, slice(*CONST[name])] = np.concatenate(halves)
    c[:, slice(*CONST["prio"])] = np.arange(E, 0, -1)
    key, query = np.meshgrid(np.arange(P), np.arange(P))
    mask = np.zeros((P, 512), np.float32)
    mask[:, 384:] = np.where(key > query, np.float32(MASKED), np.float32(0))
    c[:, slice(*CONST["mask"])] = mask
    return c


def kernel(**inputs):
    import ml_dtypes
    import numpy as np
    import concourse.bacc as _bacc
    from concourse import mybir as _mybir
    from concourse.bass_utils import run_bass_kernel_spmd as _run

    a = {k.replace("L0_attn_", "").replace("L0_ffn_", ""): np.asarray(v) for k, v in inputs.items()}
    swap = np.arange(D) ^ 1
    pack = np.zeros((P, PACK_N), np.float32)
    wide = {"Wq": a["Wq"], "Wqr": a["Wq"][:, swap], "Wk": a["Wk"], "Wkr": a["Wk"][:, swap[:32]],
            "Wvg": np.concatenate([a["Wv"], a["Wg"].T], axis=1), "bq": a["bq"][:, None], "bqr": a["bq"][swap][:, None],
            "bk": np.tile(a["bk"], 4)[:, None], "bkr": np.tile(a["bk"][swap[:32]], 4)[:, None],
            "bv": np.tile(a["bv"][None], (P, 1)), "Wo": a["Wo"], "bo": np.tile(a["bo"][None], (P, 1))}
    for name, w in wide.items():
        pack[:, slice(*PACK[name])] = w
    pack[0:E, slice(*PACK["b3"])] = a["b3"]
    wa = np.concatenate([a["W1"].transpose(0, 2, 1), a["W2"].transpose(0, 2, 1),
                         a["b1"].reshape(E, 2, P).transpose(0, 2, 1), a["b2"].reshape(E, 2, P).transpose(0, 2, 1)],
                        axis=2)
    wd = a["W3"].transpose(0, 2, 1).reshape(E, 2, P, D).transpose(0, 2, 1, 3).reshape(E, P, 2 * D)
    rows = np.zeros((2 * PARTS, HPG * T), ml_dtypes.bfloat16)
    rows[PARTS:] = -1
    arrays = {"x": a["x"], "pack": pack, "const": _tables(), "wa": wa, "wd": wd, "rows": rows}
    arrays = {f"in_{k}": np.ascontiguousarray(v) for k, v in arrays.items()}

    nc = _bacc.Bacc("TRN2", target_bir_lowering=False, num_devices=1)
    args = [nc.dram_tensor(n, v.shape, _mybir.dt.from_np(v.dtype), kind="ExternalInput").ap()
            for n, v in arrays.items()]
    args.append(nc.dram_tensor("out_x", (B, T, D), F32, kind="ExternalOutput").ap())
    attention_and_experts(nc, *args)
    return _run(nc, [arrays], core_ids=[0]).results[0]["out_x"]
```
